# Optimizing a Trainium2 kernel written in Bass

```python
import numpy as np
import jax
import jax.numpy as jnp

def _softmax(x, axis=-1):
    return jax.nn.softmax(x, axis=axis)

def _gelu(x):
    return jax.nn.gelu(x, approximate=True)

def _silu(x):
    return jax.nn.silu(x)

def _sigmoid(x):
    return jax.nn.sigmoid(x)

def _layernorm(x, axis=-1, eps=1e-05):
    m = jnp.mean(x, axis=axis, keepdims=True)
    v = jnp.var(x, axis=axis, keepdims=True)
    return (x - m) / jnp.sqrt(v + eps)

def _scatter_add(tgt, idx, src, axis=0):
    return tgt.at[idx].add(src)

def _segment_sum(src, seg, n):
    return jax.ops.segment_sum(src, seg, n)
kernel_name = 'mk_gnn_ffn_d1_gnn_r8_ac9154'

def setup_inputs(seed: int=0):
    np.random.seed(seed)
    _w = jnp.asarray

    def _rec_inputs():
        import jax
        import jax.numpy as jnp
        _gk = jax.random.key(seed)
        x = -0.0003713 + 1 * jax.random.normal(jax.random.fold_in(_gk, 1), (6250, 256), jnp.float32)
        _s = jax.random.randint(jax.random.fold_in(_gk, 2), (100000,), 0, 6250, jnp.int32)
        _d = jax.random.randint(jax.random.fold_in(_gk, 3), (100000,), 0, 6250, jnp.int32)
        _loop = jnp.arange(6250, dtype=jnp.int32)
        src = jnp.concatenate([_s, _d, _loop])
        dst = jnp.concatenate([_d, _s, _loop])
        _o = jnp.argsort(dst, stable=True)
        src = src[_o]
        dst = dst[_o]
        return (x, src, dst)
    x, src, dst = _rec_inputs()

    def _L0_gnn_setup():
        import jax, jax.numpy as jnp
        import numpy as np
        N = 6250
        E = 100000
        D = 256
        H = 256

        def _gcn_norm(edge_index, num_nodes):
            loop = jnp.arange(num_nodes)
            src = jnp.concatenate([edge_index[0], loop])
            dst = jnp.concatenate([edge_index[1], loop])
            ew = jnp.ones(src.shape[0], jnp.float32)
            deg = jax.ops.segment_sum(ew, dst, num_segments=num_nodes)
            dis = jnp.where(deg > 0, jax.lax.rsqrt(deg), 0.0)
            norm = dis[src] * ew * dis[dst]
            return (src, dst, norm)
        key = jax.random.key(seed)
        ks = jax.random.split(key, 4)
        x = jax.random.normal(ks[0], (N, D), jnp.float32)
        edge_index = jax.random.randint(ks[1], (2, E), 0, N)
        W1 = jax.random.normal(ks[2], (D, H), jnp.float32) * (1.0 / np.sqrt(D))
        b1 = jnp.zeros((H,), jnp.float32)
        W2 = jax.random.normal(ks[3], (H, H), jnp.float32) * (1.0 / np.sqrt(H))
        b2 = jnp.zeros((H,), jnp.float32)
        return {'x': x, 'edge_index': edge_index, 'W1': W1, 'b1': b1, 'W2': W2, 'b2': b2}
    _L0_gnn_all = _L0_gnn_setup()
    _L0_gnn_in = {k: v for k, v in _L0_gnn_all.items() if k in ('W1', 'b1', 'W2', 'b2')}
    del _L0_gnn_all

    def _L0_ffn_setup():
        import jax, jax.numpy as jnp
        import numpy as np
        N_EXPERTS = 8
        TOP_K = 2
        key = jax.random.key(seed)
        ks = jax.random.split(key, 5)
        B, T, C, E, H = (8, 256, 256, 8, 682)
        scale = 1.0 / np.sqrt(C)
        return {'x': jax.random.normal(ks[0], (B, T, C), dtype=jnp.float32), 'router_w': jax.random.normal(ks[1], (E, C), dtype=jnp.float32) * scale, 'w1': jax.random.normal(ks[2], (E, H, C), dtype=jnp.float32) * scale, 'w2': jax.random.normal(ks[3], (E, C, H), dtype=jnp.float32) * (1.0 / np.sqrt(H)), 'w3': jax.random.normal(ks[4], (E, H, C), dtype=jnp.float32) * scale}
    _L0_ffn_all = _L0_ffn_setup()
    _L0_ffn_in = {k: v for k, v in _L0_ffn_all.items() if k in ('router_w', 'w1', 'w2', 'w3')}
    del _L0_ffn_all
    return {'x': x, 'src': src, 'dst': dst, 'L0_gnn_W1': _L0_gnn_in['W1'], 'L0_gnn_b1': _L0_gnn_in['b1'], 'L0_gnn_W2': _L0_gnn_in['W2'], 'L0_gnn_b2': _L0_gnn_in['b2'], 'L0_ffn_router_w': _L0_ffn_in['router_w'], 'L0_ffn_w1': _L0_ffn_in['w1'], 'L0_ffn_w2': _L0_ffn_in['w2'], 'L0_ffn_w3': _L0_ffn_in['w3']}

def reference(x, src, dst, L0_gnn_W1, L0_gnn_b1, L0_gnn_W2, L0_gnn_b2, L0_ffn_router_w, L0_ffn_w1, L0_ffn_w2, L0_ffn_w3):
    import jax
    import jax.numpy as jnp

    def _L0_gnn_ref(x, edge_index, W1, b1, W2, b2):
        import jax, jax.numpy as jnp
        import numpy as np
        N = 6250
        E = 100000
        D = 256
        H = 256

        def _gcn_norm(edge_index, num_nodes):
            loop = jnp.arange(num_nodes)
            src = jnp.concatenate([edge_index[0], loop])
            dst = jnp.concatenate([edge_index[1], loop])
            ew = jnp.ones(src.shape[0], jnp.float32)
            deg = jax.ops.segment_sum(ew, dst, num_segments=num_nodes)
            dis = jnp.where(deg > 0, jax.lax.rsqrt(deg), 0.0)
            norm = dis[src] * ew * dis[dst]
            return (src, dst, norm)
        n = x.shape[0]
        src, dst, norm = _gcn_norm(edge_index, n)

        def conv(z, W, b):
            h = z @ W
            msg = h[src] * norm[:, None]
            return jax.ops.segment_sum(msg, dst, num_segments=n) + b
        z = jax.nn.relu(conv(x, W1, b1))
        z = conv(z, W2, b2)
        nrm = jnp.maximum(jnp.linalg.norm(z, axis=-1, keepdims=True), 1e-12)
        return z / nrm

    def _L0_ffn_ref(x, router_w, w1, w2, w3):
        import jax, jax.numpy as jnp
        import numpy as np
        N_EXPERTS = 8
        TOP_K = 2
        B, T, C = x.shape
        flat = x.reshape(-1, C)
        logits = flat @ router_w.T
        probs = jax.nn.softmax(logits, axis=-1)
        topk_probs, topk_idx = jax.lax.top_k(probs, TOP_K)
        topk_probs = topk_probs / (jnp.sum(topk_probs, axis=-1, keepdims=True) + 1e-09)
        onehot = jax.nn.one_hot(topk_idx, N_EXPERTS, dtype=flat.dtype)
        gates = jnp.einsum('nk,nke->ne', topk_probs, onehot)
        h1 = jnp.einsum('nc,ehc->neh', flat, w1)
        h3 = jnp.einsum('nc,ehc->neh', flat, w3)
        h = jax.nn.silu(h1) * h3
        y = jnp.einsum('neh,ech->nec', h, w2)
        out = jnp.einsum('ne,nec->nc', gates, y)
        return out.reshape(B, T, C)
    edge_index = jnp.stack([src, dst])
    x = x + _L0_gnn_ref(_layernorm(x, axis=-1), edge_index, L0_gnn_W1, L0_gnn_b1, L0_gnn_W2, L0_gnn_b2)
    x = x + _L0_ffn_ref(_layernorm(x, axis=-1)[None], L0_ffn_router_w, L0_ffn_w1, L0_ffn_w2, L0_ffn_w3)[0]
    return x

_drawn_inputs = setup_inputs


def setup_inputs(seed=0):
    import zlib

    import numpy as np

    out = dict(_drawn_inputs(seed))
    spreads = {'L0_gnn_b1': (0.0, 0.1), 'L0_gnn_b2': (0.0, 0.1)}
    factors = {}
    for name, (base, spread) in spreads.items():
        noise = np.random.default_rng([zlib.crc32(name.encode()), seed]).standard_normal(out[name].shape)
        drawn = base * np.exp(spread * noise) if base else spread * noise
        out[name] = jnp.asarray(drawn.astype(out[name].dtype))
    for name, factor in factors.items():
        out[name] = (out[name] * factor).astype(out[name].dtype)
    return out
```

```python
from contextlib import ExitStack

import numpy as np

import concourse.bass as bass
from concourse import mybir

ALU = mybir.AluOpType
ACT = mybir.ActivationFunctionType
AX = mybir.AxisListType.X
F32 = mybir.dt.float32
BF16 = mybir.dt.bfloat16
I32 = mybir.dt.int32

P = 128
N = 6250
D = 256
KC = D // P
NBLK = 50
LASTB = N // P
TAIL = N - LASTB * P
E_IN = 206250
JT = 4
SLOTS = 4
ROUNDS = 101
GROUPS = ROUNDS * SLOTS
TILES = GROUPS * JT
E_PAD = TILES * P
GP, GQ = 101, 4
assert GP * GQ == GROUPS and E_PAD >= E_IN and N < NBLK * P
LO = 64
HI = NBLK * P // LO
CT = 8
assert TILES == ROUNDS * 2 * CT

NE = 8
HID = 682
HC = 114
NHC = 6
HP = HC * NHC
HH = HP // 2
REGION = NBLK * P
NT = 106
assert NT >= (2 * N + NE * (P - 1)) // P and N + P <= REGION
EPS_LN = 1e-5


def build(nc, x, src, dst, dst_groups, W1, b1, W2, b2, router, w1, w3, w2, out):
    with ExitStack() as ctx:
        def sb(name, shape, dt=F32):
            return ctx.enter_context(nc.sbuf_tensor(name, shape, dt))

        def sem(name):
            return ctx.enter_context(nc.semaphore(name))

        def dram(name, shape, dt=F32):
            return nc.dram_tensor(name, shape, dt, kind="Internal").ap()

        U = [dram("u_layer1", (NBLK * P, D)), dram("u_layer2", (NBLK * P, D))]
        bounds_dram = dram("group_bounds", (GROUPS, 2), I32)
        dis_dram = dram("dis_rows", (NBLK, P))
        lists = dram("expert_lists", (NE * REGION, D))
        y_dram = dram("expert_rows", (NT * P, D))

        acc = sb("acc", [P, NBLK, D])
        late = sb("late", [P, NHC * NE * D])
        at = [0]

        def graph_buf(n, dt=F32):
            v = late[:, at[0]:at[0] + n]
            at[0] += n
            assert at[0] <= NHC * NE * D
            return v if dt == F32 else v.bitcast(dt)

        rows = graph_buf(SLOTS * JT * D).rearrange("p (s j d) -> p s j d", s=SLOTS, j=JT)
        src_t = graph_buf(TILES, I32)
        dst_f = graph_buf(TILES)
        gw = graph_buf(2 * KC * D).rearrange("p (l k n) -> p l k n", l=2, k=KC)
        bounds = graph_buf(2 * GROUPS, I32)[0:1, :]
        onehot = graph_buf(JT * P).rearrange("p (j n) -> p j n", j=JT)
        dst_i = rows.rearrange("p s j d -> p (s j d)")[:, 0:TILES].bitcast(I32)
        w13 = sb("w13", [P, 2, KC, NE * HP])
        cflat = w13.rearrange("p a k n -> p (a k n)")
        cat = [0]

        def count_buf(n, dt=F32):
            v = cflat[:, cat[0]:cat[0] + n]
            cat[0] += n
            return v if dt == F32 else v.bitcast(dt)

        lo_i = count_buf(TILES, I32)
        hi_i = count_buf(TILES, I32)
        lo_f = count_buf(TILES)
        hi_f = count_buf(TILES)
        gr_i = count_buf(GQ * JT * P, I32)
        hot_hi = [count_buf(CT * HI // 2, BF16).rearrange("p (t n) -> p t n", t=CT) for _ in range(2)]
        hot_lo = [count_buf(CT * LO // 2, BF16).rearrange("p (t n) -> p t n", t=CT) for _ in range(2)]
        gbi = count_buf(2 * GQ, I32)
        gbo = count_buf(2 * GQ, I32)
        count_row = count_buf(LO)
        dis_hl = count_buf(LO)
        dis_bt = count_buf(P)

        ident = sb("ident", [P, P])
        upper = sb("upper", [P, P])
        ones = sb("ones", [P, P])
        iota = sb("iota", [P, P])
        iota_b = sb("iota_b", [P, P], BF16)
        ones_b = sb("ones_b", [P, P], BF16)
        iota_i = sb("iota_i", [P, P], I32)
        part = sb("part", [P, 1])
        part_int = sb("part_int", [P, 1], I32)
        base = sb("base", [P, NBLK])
        idx_ring = sb("idx_ring", [P, SLOTS, JT], I32)
        b1col = sb("b1col", [P, KC])
        b2row = sb("b2row", [P, D])
        zs = sb("zs", [P, 2, D])
        zT = sb("zT", [P, 2, KC, P])
        dis = sb("dis", [P, NBLK])
        stats = sb("stats", [P, 6])
        mv = sb("mv", [P, 2])
        mean = sb("mean", [P, NBLK])
        var = sb("var", [P, NBLK])
        rstd = sb("rstd", [P, NBLK])
        tmp = sb("tmp", [P, NBLK])
        tick = sb("tick", [P, SLOTS])
        rw = sb("rw", [P, KC, NE])
        mask = [sb(f"mask{k}", [P, NBLK, NE]) for k in range(2)]
        red = sb("red", [P, NBLK])
        valid = sb("valid", [P, NBLK])
        gate_p = [sb(f"gate{k}", [P, NBLK]) for k in range(2)]
        pos = sb("pos", [P, NBLK, 2])
        pos_i = sb("pos_i", [P, NBLK, 2], I32)
        ring_i = sb("ring_i", [P, 2, 2], I32)
        ering = sb("ering", [P, 8, NE])
        ering_i = sb("ering_i", [P, 3, NE], I32)
        sched_i = sb("sched_i", [1, 2, NT], I32)
        xg = sb("xg", [P, 2, D])
        xT = zT
        s1 = sb("s1", [P, HP])
        h = sb("h", [P, HP])
        hT = sb("hT", [P, NHC, P])
        yb = sb("yb", [P, 2, D])

        def router_buf(flat):
            return flat[:, 0:NBLK * NE].rearrange("p (b e) -> p b e", e=NE)

        logits = router_buf(s1[:])
        prob = router_buf(h[:])
        work = router_buf(hT.rearrange("p c n -> p (c n)"))
        totals = [router_buf(xg.rearrange("p r d -> p (r d)")), router_buf(zT.rearrange("p r k n -> p (r k n)"))]
        sched = s1[0:1, 0:5 * NT].rearrange("p (q t) -> p q t", q=5)
        w2s = late.rearrange("p (c n) -> p c n", c=NHC)
        ps = ctx.enter_context(nc.psum_tensor("ps", [P, 8, 512], F32))

        psT = [ps[:, r, 0:KC * P].rearrange("p (k n) -> p k n", k=KC) for r in range(2)]
        psM = [ps[:, 2 + r, 0:D] for r in range(2)]
        psAgg = ps[:, 4, 0:D]
        psCnt = ps[0:HI, 5, 0:LO]
        psWithin = ps[:, 4, 0:NBLK * NE].rearrange("p (b e) -> p b e", e=NE)
        psTotal = ps[:, 5, 0:NBLK * NE].rearrange("p (b e) -> p b e", e=NE)
        psDis = ps[:, 6, 0:NBLK]

        weights_loaded = sem("weights_loaded")
        edges_loaded = sem("edges_loaded")
        groups_loaded = sem("groups_loaded")
        src_loaded = sem("src_loaded")
        pad_zeroed = sem("pad_zeroed")
        x_loaded = sem("x_loaded")
        iotas_made = sem("iotas_made")
        consts_made = sem("consts_made")
        dve_step = sem("dve_step")
        gate_passed = sem("gate_passed")
        hots_ready = sem("hots_ready")
        hots_counted = sem("hots_counted")
        bounds_made = sem("bounds_made")
        bounds_stored = sem("bounds_stored")
        bounds_loaded = sem("bounds_loaded")
        dis_made = sem("dis_made")
        dis_stored = sem("dis_stored")
        dis_back = sem("dis_back")
        dis_turned = sem("dis_turned")
        dis_ready = sem("dis_ready")
        root_asked = sem("root_asked")
        root_taken = sem("root_taken")
        z_scaled = sem("z_scaled")
        z_turned = sem("z_turned")
        zT_ready = sem("zT_ready")
        z_times_w = sem("z_times_w")
        product_out = sem("product_out")
        u_stored = [sem(f"u_stored{r}") for r in range(2)]
        idx_staged = [sem(f"idx_staged{r}") for r in range(SLOTS)]
        rows_landed = [sem(f"rows_landed{r}") for r in range(SLOTS)]
        slot_free = [sem(f"slot_free{r}") for r in range(SLOTS)]
        onehot_ready = sem("onehot_ready")
        onehot_used = sem("onehot_used")
        agg_added = sem("agg_added")
        graph_over = sem("graph_over")
        x_again = [sem(f"x_again{r}") for r in range(2)]
        x_used = sem("x_used")
        w13_loaded = sem("w13_loaded")
        w2_loaded = sem("w2_loaded")
        exp_asked = sem("exp_asked")
        exp_made = sem("exp_made")
        mask_ready = sem("mask_ready")
        ranks_made = sem("ranks_made")
        fill_ready = sem("fill_ready")
        scatter_ready = sem("scatter_ready")
        scattered = [sem(f"scattered{r}") for r in range(2)]
        sched_ready = sem("sched_ready")
        tile_loaded = [sem(f"tile_loaded{r}") for r in range(2)]
        tile_turned = sem("tile_turned")
        xT_ready = sem("xT_ready")
        hidden_made = sem("hidden_made")
        silu_made = sem("silu_made")
        h_ready = sem("h_ready")
        h_turned = sem("h_turned")
        hT_ready = sem("hT_ready")
        y_made = sem("y_made")
        y_ready = sem("y_ready")
        yb_written = [sem(f"yb_written{r}") for r in range(2)]
        comb_ready = sem("comb_ready")
        y_back = [sem(f"y_back{r}") for r in range(2)]
        out_ready = sem("out_ready")
        out_stored = [sem(f"out_stored{r}") for r in range(2)]

        def gate(eng, s, value):
            eng.wait_ge(s, value)
            eng.sem_inc(gate_passed, 1)

        def dram_block(t, n_blocks, i, r):
            v = t[0:n_blocks * P, :].rearrange("(i r p) d -> i r p d", r=2, p=P)
            return v[bass.ds(i, 1), r].rearrange("a p d -> (a p) d")

        def acc_block(b):
            return acc[:, bass.ds(b, 1), :].rearrange("p a d -> p (a d)")

        block = ctx.enter_context(nc.Block())

        @block.sync
        def _(sp):
            sp.dma_start(dst_i, dst).then_inc(edges_loaded, 16)
            sp.dma_start(gr_i[0:GP, :], dst_groups).then_inc(groups_loaded, 16)
            sp.wait_ge(pad_zeroed, 1)
            sp.dma_start(acc[:, 0:LASTB, :], x[0:LASTB * P, :].rearrange("(b p) d -> p b d", p=P)).then_inc(x_loaded, 16)
            sp.dma_start(acc[0:TAIL, LASTB, :], x[LASTB * P:N, :]).then_inc(x_loaded, 16)
            for k, w in enumerate((W1, W2)):
                sp.dma_start(gw[:, k], w.rearrange("(k p) n -> p k n", p=P)).then_inc(weights_loaded, 16)
            sp.dma_start(b1col[:], b1).then_inc(weights_loaded, 16)
            sp.dma_start(b2row[:], b2.to_broadcast([P, D])).then_inc(weights_loaded, 16)
            sp.dma_start(rw[:], router.rearrange("(k p) e -> p k e", p=P)).then_inc(weights_loaded, 16)
            sp.dma_start(src_t, src).then_inc(src_loaded, 16)
            sp.wait_ge(bounds_made, 1)
            sp.dma_start(bounds_dram.rearrange("(p q) c -> p (q c)", q=GQ), gbo[0:GP, :]).then_inc(bounds_stored, 16)
            sp.wait_ge(bounds_stored, 16)
            sp.dma_start(bounds, bounds_dram.rearrange("(a g) c -> a (g c)", a=1)).then_inc(bounds_loaded, 16)
            sp.wait_ge(dis_made, 1)
            sp.dma_start(dis_dram.rearrange("b (c n) -> (b c) n", n=LO), dis_hl[0:HI, :]).then_inc(dis_stored, 16)
            sp.wait_ge(dis_stored, 16)
            sp.dma_start(dis_bt[0:NBLK, :], dis_dram).then_inc(dis_back, 16)
            for layer in range(2):
                with sp.Fori(0, NBLK // 2, 1) as i:
                    for r in range(2):
                        sp.wait_ge(product_out, 2 * i + (NBLK * layer + r + 3))
                        sp.dma_start(dram_block(U[layer], NBLK, i, r), acc_block(2 * i + r)).then_inc(u_stored[r], 16)
                if layer == 0:
                    for a, w in enumerate((w1, w3)):
                        sp.dma_start(w13[:, a], w.rearrange("(k p) n -> p k n", p=P)).then_inc(w13_loaded, 16)
            with sp.Fori(0, LASTB // 2, 1) as i:
                for r in range(2):
                    sp.wait_ge(x_used, 2 * i + (r + 1))
                    sp.dma_start(xg[:, r], dram_block(x, LASTB, i, r)).then_inc(x_again[r], 16)
            sp.wait_ge(x_used, LASTB + 1)
            sp.dma_start(xg[0:TAIL, 0], x[LASTB * P:N, :]).then_inc(x_again[0], 16)
            sp.wait_ge(graph_over, 1)
            sp.dma_start(w2s[0:HC], w2.rearrange("(c p) n -> p c n", p=HC)).then_inc(w2_loaded, 16)
            sp.wait_ge(sched_ready, 1)
            sp.wait_ge(scattered[0], 32 * (LASTB // 2 + 1))
            sp.wait_ge(scattered[1], 32 * (LASTB // 2))
            for r in range(2):
                sp.wait_ge(yb_written[r], 16 * NE // 2)
            with sp.Fori(0, NT // 2, 1) as i:
                for r in range(2):
                    row = sp.value_load(sched_i[0:1, 1, bass.ds(2 * i + r, 1)], min_val=0, max_val=NE * REGION - P)
                    sp.wait_ge(tile_turned, 2 * i + (r + 1))
                    sp.dma_start(xg[:, r], lists[bass.ds(row, P), :]).then_inc(tile_loaded[r], 16)
            with sp.Fori(0, LASTB // 2, 1) as i:
                for r in range(2):
                    sp.wait_ge(out_ready, 2 * i + (r + 1))
                    sp.dma_start(dram_block(out, LASTB, i, r), acc_block(2 * i + r)).then_inc(out_stored[r], 16)
            sp.wait_ge(out_ready, LASTB + 1)
            sp.dma_start(out[LASTB * P:N, :], acc[0:TAIL, LASTB, :]).then_inc(out_stored[0], 16)
            sp.wait_ge(out_stored[0], 16 * (LASTB // 2 + 1))
            sp.wait_ge(out_stored[1], 16 * (LASTB // 2))

        @block.gpsimd
        def _(pool):
            nc.gpsimd.iota(iota_i[:], pattern=[[1, P]], base=0, channel_multiplier=0).then_inc(iotas_made, 1)
            nc.gpsimd.iota(part_int[:], pattern=[[0, 1]], base=0, channel_multiplier=1).then_inc(iotas_made, 1)
            for layer in range(2):
                for r in range(2):
                    pool.wait_ge(u_stored[r], 16 * (NBLK // 2) * (layer + 1))
                with pool.Fori(0, ROUNDS, 1) as k:
                    for r in range(SLOTS):
                        gate(pool, idx_staged[r], k + (layer * ROUNDS + 1))
                        for j in range(JT):
                            pool.indirect_dma_start(out=rows[:, r, j], out_offset=None, in_=U[layer],
                                                    in_offset=bass.IndirectOffsetOnAxis(ap=idx_ring[:, r, j:j + 1], axis=0)).then_inc(rows_landed[r], 16)
            pool.wait_ge(fill_ready, 1)
            for e in range(NE):
                pool.indirect_dma_start(out=lists, out_offset=bass.IndirectOffsetOnAxis(ap=ering_i[:, 0, e:e + 1], axis=0),
                                        in_=yb[:, e % 2], in_offset=None).then_inc(yb_written[e % 2], 16)
            with pool.Fori(0, LASTB // 2, 1) as i:
                for r in range(2):
                    gate(pool, scatter_ready, 2 * i + (r + 1))
                    for k in range(2):
                        pool.indirect_dma_start(out=lists, out_offset=bass.IndirectOffsetOnAxis(ap=ring_i[:, r, k:k + 1], axis=0),
                                                in_=zs[:, r], in_offset=None).then_inc(scattered[r], 16)
            pool.wait_ge(scatter_ready, LASTB + 1)
            for k in range(2):
                pool.indirect_dma_start(out=lists, out_offset=bass.IndirectOffsetOnAxis(ap=ring_i[0:TAIL, 0, k:k + 1], axis=0),
                                        in_=zs[0:TAIL, 0], in_offset=None).then_inc(scattered[0], 16)
            with pool.Fori(0, NT // 2, 1) as i:
                for r in range(2):
                    gate(pool, y_ready, 2 * i + (r + 2))
                    pool.dma_start(dram_block(y_dram, NT, i, r), yb[:, r]).then_inc(yb_written[r], 16)
            for r in range(2):
                pool.wait_ge(yb_written[r], 16 * (NT // 2 + NE // 2))
            with pool.Fori(0, NBLK // 2, 1) as i:
                for r in range(2):
                    gate(pool, comb_ready, 2 * i + (r + 1))
                    for k in range(2):
                        pool.indirect_dma_start(out=(xg, zs)[k][:, r], out_offset=None, in_=y_dram,
                                                in_offset=bass.IndirectOffsetOnAxis(ap=ring_i[:, r, k:k + 1], axis=0)).then_inc(y_back[r], 16)

        @block.scalar
        def _(act):
            act.sem_inc(xT_ready, 1)

            def root(n, to, of):
                act.wait_ge(root_asked, n)
                nc.scalar.activation(to, of, ACT.Sqrt).then_inc(root_taken, 1)

            root(1, dis_hl[0:HI, :], count_row[0:HI, :])
            root(2, rstd[:], tmp[:])
            act.wait_ge(weights_loaded, 16 * 5)
            act.wait_ge(dis_ready, 1)
            act.wait_ge(src_loaded, 16)
            for layer in range(3):
                if layer == 2:
                    root(3, rstd[:], tmp[:])
                    root(4, rstd[:], tmp[:])
                with act.Fori(0, NBLK // 2, 1) as i:
                    for r in range(2):
                        gate(act, z_turned, 2 * i + (NBLK * layer + r + 3))
                        if layer == 1:
                            for k in range(KC):
                                ins = nc.scalar.activation(zT[:, r, k], psT[r][:, k], ACT.Relu, bias=b1col[:, k:k + 1])
                            ins.then_inc(zT_ready, 1)
                        else:
                            nc.scalar.copy(zT[:, r], psT[r]).then_inc(zT_ready, 1)
                    for r in range(2):
                        gate(act, z_times_w, 2 * i + (NBLK * layer + r + 1))
                        if layer == 2:
                            nc.scalar.copy(logits[:, bass.ds(2 * i + r, 1), :].rearrange("p a e -> p (a e)"), psM[r][:, 0:NE]).then_inc(product_out, 1)
                        else:
                            nc.scalar.activation(acc_block(2 * i + r), psM[r], ACT.Copy, scale=dis[:, bass.ds(2 * i + r, 1)]).then_inc(product_out, 1)
                if layer < 2:
                    with act.Fori(0, ROUNDS, 1) as k:
                        for r in range(SLOTS):
                            gate(act, slot_free[r], k + (layer * ROUNDS + 1))
                            nc.scalar.copy(idx_ring[:, r, :], src_t[:, bass.ds((k * SLOTS + r) * JT, JT)]).then_inc(idx_staged[r], 1)
            act.wait_ge(exp_asked, 1)
            nc.scalar.activation(prob, work, ACT.Exp).then_inc(exp_made, 1)

            def silu(n):
                gate(act, hidden_made, n + 1)
                gate(act, h_ready, n + 1)
                nc.scalar.activation(s1.rearrange("p (c n) -> p c n", c=2), ps[:, 0:2, 0:HH], ACT.Silu).then_inc(silu_made, 1)

            def turned_out(r, n):
                gate(act, tile_turned, n + 3)
                nc.scalar.copy(xT[:, r], ps[:, 7, 0:KC * P].rearrange("p (k n) -> p k n", k=KC)).then_inc(xT_ready, 1)

            turned_out(0, 0)
            with act.Fori(0, NT // 2 - 1, 1) as i:
                silu(2 * i)
                turned_out(1, 2 * i + 1)
                silu(2 * i + 1)
                turned_out(0, 2 * i + 2)
            silu(NT - 2)
            turned_out(1, NT - 1)
            silu(NT - 1)

        @block.tensor
        def _(pe):
            pe.sem_inc(hots_counted, 2)
            pe.sem_inc(onehot_used, JT)
            pe.sem_inc(z_turned, 2)
            pe.sem_inc(tile_turned, 2)
            pe.sem_inc(h_turned, 1)
            pe.sem_inc(y_made, 1)
            pe.wait_ge(consts_made, 1)
            nc.tensor.matmul(psCnt, ones_b[0:1, 0:HI], ones_b[0:1, 0:LO], start=True, stop=True, skip_group_check=True)
            with pe.Fori(0, ROUNDS, 1) as i:
                for r in range(2):
                    pe.wait_ge(hots_ready, 2 * i + (r + 1))
                    for t in range(CT):
                        mm = nc.tensor.matmul(psCnt, hot_hi[r][:, t], hot_lo[r][:, t], start=False, stop=True, skip_group_check=True)
                    mm.then_inc(hots_counted, 1)
            pe.wait_ge(dis_back, 16)
            nc.tensor.transpose(psDis, dis_bt[0:NBLK, :], ident[0:NBLK, 0:NBLK]).then_inc(dis_turned, 1)
            pe.wait_ge(weights_loaded, 16 * 5)
            steps = pe.alloc_register("pe_steps")
            pe.reg_mov(steps, 0)
            for layer in range(3):
                w = (gw[:, 0], gw[:, 1], rw[:])[layer]
                with pe.Fori(0, NBLK // 2, 1) as i:
                    for r in range(2):
                        pe.wait_ge(z_scaled, 2 * i + (NBLK * layer + r + 1))
                        for k in range(KC):
                            mm = nc.tensor.transpose(psT[r][:, k], zs[:, r, k * P:(k + 1) * P], ident[:])
                        mm.then_inc(z_turned, 1)
                    for r in range(2):
                        pe.wait_ge(zT_ready, 2 * i + (NBLK * layer + r + 1))
                        pe.wait_ge(product_out, 2 * i + (NBLK * layer + r + 1))
                        for k in range(KC):
                            mm = nc.tensor.matmul(psM[r][:, 0:NE] if layer == 2 else psM[r], zT[:, r, k], w[:, k],
                                                  start=k == 0, stop=k == KC - 1)
                        mm.then_inc(z_times_w, 1)
                if layer == 2:
                    break
                pe.wait_ge(bounds_loaded, 16)
                with pe.Fori(0, ROUNDS, 1) as k:
                    for r in range(SLOTS):
                        first = pe.value_load(bounds[0:1, bass.ds((k * SLOTS + r) * 2, 1)], min_val=0, max_val=NBLK - 1)
                        end = pe.value_load(bounds[0:1, bass.ds((k * SLOTS + r) * 2 + 1, 1)], min_val=1, max_val=NBLK)
                        gate(pe, rows_landed[r], k * (16 * JT) + 16 * JT * (layer * ROUNDS + 1))
                        with pe.Fori(first, end, 1):
                            n = pe.snap(steps)
                            pe.wait_ge(agg_added, n + 1)
                            for j in range(JT):
                                pe.wait_ge(onehot_ready, n * JT + (j + 1))
                                nc.tensor.matmul(psAgg, onehot[:, j], rows[:, r, j], start=j == 0, stop=j == JT - 1).then_inc(onehot_used, 1)
                            pe.reg_add(steps, steps, 1)
            pe.wait_ge(mask_ready, 1)
            flat = work.rearrange("p b e -> p (b e)")
            nc.tensor.matmul(ps[:, 4, 0:NBLK * NE], upper[:], flat, start=True, stop=True)
            nc.tensor.matmul(ps[:, 5, 0:NBLK * NE], ones[:], flat, start=True, stop=True).then_inc(ranks_made, 1)

            def turn_tile(r, i, n):
                pe.wait_ge(tile_loaded[r], i * 16 + 16)
                pe.wait_ge(xT_ready, n + 1)
                for k in range(KC):
                    mm = nc.tensor.transpose(ps[:, 7, k * P:(k + 1) * P], xg[:, r, k * P:(k + 1) * P], ident[:])
                mm.then_inc(tile_turned, 1)

            def expert_of(n):
                return pe.value_load(sched_i[0:1, 0, bass.ds(n, 1)], min_val=0, max_val=NE - 1)

            def hidden(r, n):
                e = expert_of(n)
                pe.wait_ge(xT_ready, n + 2)
                pe.wait_ge(h_ready, n + 1)
                for a in range(2):
                    for c in range(2):
                        for k in range(KC):
                            mm = nc.tensor.matmul(ps[:, 2 * a + c, 0:HH], xT[:, r, k],
                                                  w13[:, a, k, bass.ds(e * HP + c * HH, HH)], start=k == 0, stop=k == KC - 1)
                mm.then_inc(hidden_made, 1)

            def turn_h(r, n):
                pe.wait_ge(h_ready, n + 2)
                pe.wait_ge(hT_ready, n + 1)
                for c in range(NHC):
                    mm = nc.tensor.transpose(ps[0:HC, 4 + c // 3, (c % 3) * P:(c % 3 + 1) * P], h[:, c * HC:(c + 1) * HC], ident[:])
                mm.then_inc(h_turned, 1)

            def out_rows(r, n):
                e = expert_of(n)
                pe.wait_ge(hT_ready, n + 2)
                pe.wait_ge(y_ready, n + 1)
                for c in range(NHC):
                    mm = nc.tensor.matmul(ps[:, 6, 0:D], hT[0:HC, c, :], w2s[0:HC, c, bass.ds(e * D, D)], start=c == 0, stop=c == NHC - 1)
                mm.then_inc(y_made, 1)

            pe.wait_ge(sched_ready, 1)
            pe.wait_ge(w13_loaded, 32)
            pe.wait_ge(w2_loaded, 16)
            turn_tile(0, 0, 0)
            hidden(0, 0)
            turn_tile(1, 0, 1)
            with pe.Fori(0, NT // 2 - 1, 1) as i:
                hidden(1, 2 * i + 1)
                turn_h(0, 2 * i)
                turn_tile(0, i + 1, 2 * i + 2)
                out_rows(0, 2 * i)
                hidden(0, 2 * i + 2)
                turn_h(1, 2 * i + 1)
                turn_tile(1, i + 1, 2 * i + 3)
                out_rows(1, 2 * i + 1)
            hidden(1, NT - 1)
            for n in (NT - 2, NT - 1):
                turn_h(n % 2, n)
                out_rows(n % 2, n)

        @block.vector
        def _(dve):
            v = nc.vector
            dve.sem_inc(agg_added, 1)
            dve.sem_inc(product_out, 2)
            dve.sem_inc(x_used, 2)
            dve.sem_inc(h_ready, 1)
            dve.sem_inc(hT_ready, 1)
            dve.sem_inc(y_ready, 1)
            for r in range(SLOTS):
                dve.sem_inc(slot_free[r], 1)

            done = [0]

            def then(ins):
                ins.then_inc(dve_step, 1)
                done[0] += 1
                dve.wait_ge(dve_step, done[0])

            def then_in(ins, i, n_per, q):
                ins.then_inc(dve_step, 1)
                gate(dve, dve_step, i * n_per + (done[0] + q + 1))

            v.memset(acc[:, LASTB:NBLK, :], 0.0).then_inc(pad_zeroed, 1)
            v.memset(ones[:], 1.0)
            then(v.memset(ones_b[:], 1.0))
            dve.wait_ge(iotas_made, 2)
            v.tensor_copy(iota[:], iota_i[:])
            v.tensor_copy(iota_b[:], iota_i[:])
            then(v.tensor_copy(part[:], part_int[:]))
            v.tensor_scalar(ident[:], iota[:], part[:, 0:1], None, ALU.is_equal)
            v.tensor_scalar(upper[:], iota[:], part[:, 0:1], None, ALU.is_gt)
            then(v.tensor_scalar(base[:], iota[:, 0:NBLK], float(P), None, ALU.mult))
            v.tensor_scalar(valid[:], base[:], part[:, 0:1], float(N), ALU.add, ALU.is_lt).then_inc(consts_made, 1)
            dve.wait_ge(edges_loaded, 16)
            v.tensor_copy(dst_f, dst_i)
            v.tensor_scalar(lo_i, dst_i, LO - 1, None, ALU.bitwise_and)
            then(v.tensor_scalar(hi_i, dst_i, 6, None, ALU.logical_shift_right))
            v.tensor_copy(lo_f, lo_i)
            then(v.tensor_copy(hi_f, hi_i))
            for_hi = iota_b[:, 0:HI].unsqueeze(1).to_broadcast([P, CT, HI])
            for_lo = iota_b[:, 0:LO].unsqueeze(1).to_broadcast([P, CT, LO])
            with dve.Fori(0, ROUNDS, 1) as i:
                for r in range(2):
                    gate(dve, hots_counted, 2 * i + (r + 1))
                    v.tensor_tensor(hot_hi[r], hi_f[:, bass.ds((2 * i + r) * CT, CT)].unsqueeze(2).to_broadcast([P, CT, HI]),
                                    for_hi, ALU.is_equal)
                    v.tensor_tensor(hot_lo[r], lo_f[:, bass.ds((2 * i + r) * CT, CT)].unsqueeze(2).to_broadcast([P, CT, LO]),
                                    for_lo, ALU.is_equal).then_inc(hots_ready, 1)
            dve.wait_ge(groups_loaded, 16)
            gr = gr_i[0:GP, :].rearrange("p (q e) -> p q e", q=GQ)
            v.tensor_reduce(gbi[0:GP, 0:GQ], gr, AX, ALU.min)
            then(v.tensor_reduce(gbi[0:GP, GQ:2 * GQ], gr, AX, ALU.max))
            then(v.tensor_scalar(gbi[0:GP, :], gbi[0:GP, :], 7, None, ALU.logical_shift_right))
            pair = gbo[0:GP, :].rearrange("p (q c) -> p q c", c=2)
            v.tensor_copy(pair[:, :, 0], gbi[0:GP, 0:GQ])
            v.tensor_scalar(pair[:, :, 1], gbi[0:GP, GQ:2 * GQ], 1, None, ALU.add).then_inc(bounds_made, 1)
            dve.wait_ge(hots_counted, 2 + 2 * ROUNDS)
            v.tensor_copy(count_row[0:HI, :], psCnt).then_inc(root_asked, 1)
            dve.wait_ge(root_taken, 1)
            v.reciprocal(dis_hl[0:HI, :], dis_hl[0:HI, :]).then_inc(dis_made, 1)
            dve.wait_ge(x_loaded, 32)

            def moments(b, i, n_per, q):
                then_in(v.bn_stats(stats[:], acc_block(b)), i, n_per, q)
                then_in(v.bn_aggr(mv[:], stats[:]), i, n_per, q + 1)
                v.tensor_copy(mean[:, bass.ds(b, 1)], mv[:, 0:1])
                then_in(v.tensor_copy(var[:, bass.ds(b, 1)], mv[:, 1:2]), i, n_per, q + 2)

            def one_over_std(n):
                then(v.tensor_scalar(tmp[:], var[:], EPS_LN, None, ALU.add))
                v.tensor_copy(tick[:, 0:1], tmp[:, 0:1]).then_inc(root_asked, 1)
                dve.wait_ge(root_taken, n)
                then(v.reciprocal(rstd[:], rstd[:]))

            with dve.Fori(0, NBLK, 1) as b:
                moments(b, b, 3, 0)
            done[0] += 3 * NBLK
            one_over_std(2)
            dve.wait_ge(dis_turned, 1)
            v.tensor_copy(dis[:], psDis).then_inc(dis_ready, 1)
            dve.wait_ge(weights_loaded, 16 * 5)
            steps = dve.alloc_register("dve_steps")
            dve.reg_mov(steps, 0)
            for layer in range(3):
                if layer == 2:
                    with dve.Fori(0, NBLK, 1) as b:
                        then_in(v.scalar_tensor_tensor(acc_block(b), acc_block(b), dis[:, bass.ds(b, 1)], b2row[:], ALU.mult, ALU.add), b, 4, 0)
                        moments(b, b, 4, 1)
                    done[0] += 4 * NBLK
                    then(v.tensor_tensor(tmp[:], mean[:], mean[:], ALU.mult))
                    then(v.tensor_tensor(tmp[:], tmp[:], var[:], ALU.add))
                    v.tensor_scalar(tmp[:], tmp[:], float(D), None, ALU.mult).then_inc(root_asked, 1)
                    dve.wait_ge(root_taken, 3)
                    then(v.tensor_scalar(rstd[:], rstd[:], 1e-12, None, ALU.max))
                    then(v.reciprocal(red[:], rstd[:]))
                    with dve.Fori(0, LASTB // 2, 1) as i:
                        for r in range(2):
                            gate(dve, x_again[r], i * 16 + 16)
                            ins = v.scalar_tensor_tensor(acc_block(2 * i + r), acc_block(2 * i + r), red[:, bass.ds(2 * i + r, 1)], xg[:, r], ALU.mult, ALU.add)
                            ins.then_inc(x_used, 1)
                            gate(dve, x_used, 2 * i + (r + 3))
                            moments(2 * i + r, i, 6, 3 * r)
                    done[0] += 3 * LASTB
                    dve.wait_ge(x_again[0], 16 * (LASTB // 2 + 1))
                    then(v.scalar_tensor_tensor(acc[0:TAIL, LASTB, :], acc[0:TAIL, LASTB, :], red[0:TAIL, LASTB:LASTB + 1], xg[0:TAIL, 0], ALU.mult, ALU.add))
                    then(v.bn_stats(stats[:], acc[:, LASTB, :]))
                    then(v.bn_aggr(mv[:], stats[:]))
                    v.tensor_copy(mean[:, LASTB:LASTB + 1], mv[:, 0:1])
                    then(v.tensor_copy(var[:, LASTB:LASTB + 1], mv[:, 1:2]))
                    one_over_std(4)
                with dve.Fori(0, NBLK // 2, 1) as i:
                    for r in range(2):
                        b = 2 * i + r
                        gate(dve, z_turned, 2 * i + (NBLK * layer + r + 1))
                        if layer == 1:
                            v.tensor_scalar(zs[:, r], acc_block(b), dis[:, bass.ds(b, 1)], None, ALU.mult).then_inc(z_scaled, 1)
                        else:
                            v.tensor_scalar(zs[:, r], acc_block(b), mean[:, bass.ds(b, 1)], rstd[:, bass.ds(b, 1)], ALU.subtract, ALU.mult).then_inc(z_scaled, 1)
                if layer == 2:
                    break
                dve.wait_ge(bounds_loaded, 16)
                with dve.Fori(0, ROUNDS, 1) as k:
                    for r in range(SLOTS):
                        first = dve.value_load(bounds[0:1, bass.ds((k * SLOTS + r) * 2, 1)], min_val=0, max_val=NBLK - 1)
                        end = dve.value_load(bounds[0:1, bass.ds((k * SLOTS + r) * 2 + 1, 1)], min_val=1, max_val=NBLK)
                        with dve.Fori(first, end, 1) as b:
                            n = dve.snap(steps)
                            for j in range(JT):
                                dve.wait_ge(onehot_used, n * JT + (j + 1))
                                v.tensor_scalar(onehot[:, j], iota[:], base[:, bass.ds(b, 1)],
                                                dst_f[:, bass.ds((k * SLOTS + r) * JT + j, 1)], ALU.add, ALU.is_equal).then_inc(onehot_ready, 1)
                            gate(dve, onehot_used, n * JT + 2 * JT)
                            gate(dve, agg_added, n + 1)
                            v.tensor_tensor(acc_block(b), acc_block(b), psAgg, ALU.add).then_inc(agg_added, 1)
                            dve.reg_add(steps, steps, 1)
                        v.memset(tick[:, r:r + 1], 0.0).then_inc(slot_free[r], 1)
                gate(dve, agg_added, dve.snap(steps) + 1)
                if layer == 1:
                    v.memset(tick[:, 0:1], 0.0).then_inc(graph_over, 1)

            dve.wait_ge(product_out, 2 + 3 * NBLK)

            def by_token(t):
                return t.unsqueeze(2).to_broadcast([P, NBLK, NE])

            def by_expert(t):
                return t.unsqueeze(1).to_broadcast([P, NBLK, NE])

            e_iota = by_expert(iota[:, 0:NE])
            then(v.tensor_reduce(red[:], logits, AX, ALU.max))
            v.tensor_tensor(work, logits, by_token(red[:]), ALU.subtract).then_inc(exp_asked, 1)
            dve.wait_ge(exp_made, 1)
            then(v.tensor_reduce(red[:], prob, AX, ALU.add))
            then(v.reciprocal(red[:], red[:]))
            then(v.tensor_tensor(prob, prob, by_token(red[:]), ALU.mult))
            for k in range(2):
                then(v.tensor_reduce(gate_p[k][:], prob, AX, ALU.max))
                then(v.tensor_tensor(work, prob, by_token(gate_p[k][:]), ALU.is_equal))
                then(v.scalar_tensor_tensor(work, work, float(-NE), e_iota, ALU.mult, ALU.add))
                then(v.tensor_reduce(red[:], work, AX, ALU.min))
                then(v.tensor_tensor(mask[k][:], work, by_token(red[:]), ALU.is_equal))
                if k == 0:
                    then(v.scalar_tensor_tensor(prob, mask[0][:], -2.0, prob, ALU.mult, ALU.add))
            then(v.tensor_tensor(red[:], gate_p[0][:], gate_p[1][:], ALU.add))
            then(v.tensor_scalar(red[:], red[:], 1e-9, None, ALU.add))
            then(v.reciprocal(red[:], red[:]))
            for k in range(2):
                v.tensor_tensor(gate_p[k][:], gate_p[k][:], red[:], ALU.mult)
                then(v.tensor_tensor(mask[k][:], mask[k][:], by_token(valid[:]), ALU.mult))
            v.tensor_tensor(work, mask[0][:], mask[1][:], ALU.add).then_inc(mask_ready, 1)
            v.memset(yb[:], 0.0)
            dve.wait_ge(ranks_made, 1)
            then(v.tensor_copy(totals[0][:], psTotal))
            cur, reach = 0, 1
            while reach < NBLK:
                v.tensor_copy(totals[1 - cur][:, 0:reach], totals[cur][:, 0:reach])
                then(v.tensor_tensor(totals[1 - cur][:, reach:], totals[cur][:, reach:], totals[cur][:, :NBLK - reach], ALU.add))
                cur, reach = 1 - cur, 2 * reach
            scan = totals[cur]
            count = scan[:, NBLK - 1, :]
            first_row = ering[:, 0, :]
            then(v.tensor_scalar(first_row, iota[:, 0:NE], float(REGION), None, ALU.mult))
            then(v.tensor_tensor(ering[:, 1, :], count, first_row, ALU.add))
            v.tensor_scalar(ering_i[:, 0, :], ering[:, 1, :], part[:, 0:1], None, ALU.add).then_inc(fill_ready, 1)
            then(v.tensor_tensor(work, psWithin, scan, ALU.add))
            then(v.tensor_tensor(work, work, psTotal, ALU.subtract))
            then(v.tensor_tensor(work, work, by_expert(first_row), ALU.add))
            for k in range(2):
                then(v.tensor_tensor(prob, mask[k][:], work, ALU.mult))
                then(v.tensor_reduce(pos[:, :, k], prob, AX, ALU.add))
            then(v.tensor_copy(pos_i[:], pos[:]))

            def for_scatter(b, r):
                v.tensor_scalar(zs[:, r], acc_block(b), mean[:, bass.ds(b, 1)], rstd[:, bass.ds(b, 1)], ALU.subtract, ALU.mult)
                v.tensor_copy(ring_i[:, r, :], pos_i[:, bass.ds(b, 1), :].rearrange("p a k -> p (a k)")).then_inc(scatter_ready, 1)

            for r in range(2):
                for_scatter(r, r)
            with dve.Fori(1, LASTB // 2, 1) as i:
                for r in range(2):
                    gate(dve, scattered[r], i * 32)
                    for_scatter(2 * i + r, r)
            dve.wait_ge(scattered[0], 32 * (LASTB // 2))
            for_scatter(LASTB, 0)

            tiles, ends, shift = ering[:, 2, :], ering[:, 3, :], ering[:, 4, :]
            then(v.tensor_scalar(ering_i[:, 1, :], count, float(P - 1), None, ALU.add))
            then(v.tensor_scalar(ering_i[:, 2, :], ering_i[:, 1, :], 7, None, ALU.logical_shift_right))
            then(v.tensor_copy(tiles, ering_i[:, 2, :]))
            then(v.tensor_copy(ends, tiles))
            for e in range(1, NE):
                then(v.tensor_tensor(ends[:, e:e + 1], ends[:, e - 1:e], tiles[:, e:e + 1], ALU.add))
            tile_no, expert, rel, flag, taken = (sched[:, q, :] for q in range(5))
            then(v.tensor_scalar(taken[:, 0:1], ends[0:1, NE - 1:NE], -1.0, None, ALU.add))
            then(v.tensor_scalar(tile_no, iota[0:1, 0:NT], taken[:, 0:1], None, ALU.min))
            v.tensor_copy(rel, tile_no)
            then(v.memset(expert, 0.0))
            for e in range(NE - 1):
                v.tensor_scalar(flag, tile_no, ends[0:1, e:e + 1], None, ALU.is_ge)
                then(v.tensor_scalar(taken, tile_no, ends[0:1, e:e + 1], tiles[0:1, e:e + 1], ALU.is_ge, ALU.mult))
                v.tensor_tensor(expert, expert, flag, ALU.add)
                then(v.tensor_tensor(rel, rel, taken, ALU.subtract))
            v.tensor_copy(sched_i[:, 0, :], expert)
            then(v.tensor_scalar(rel, rel, float(P), None, ALU.mult))
            then(v.scalar_tensor_tensor(flag, expert, float(REGION), rel, ALU.mult, ALU.add))
            v.tensor_copy(sched_i[:, 1, :], flag).then_inc(sched_ready, 1)
            then(v.tensor_tensor(shift, ends, tiles, ALU.subtract))
            then(v.scalar_tensor_tensor(shift, shift, float(P), first_row, ALU.mult, ALU.subtract))
            for k in range(2):
                then(v.tensor_tensor(prob, mask[k][:], by_expert(shift), ALU.mult))
                then(v.tensor_reduce(red[:], prob, AX, ALU.add))
                then(v.tensor_tensor(pos[:, :, k], pos[:, :, k], red[:], ALU.add))
            then(v.tensor_copy(pos_i[:], pos[:]))

            def product(r, n):
                gate(dve, silu_made, n + 1)
                gate(dve, h_turned, n + 1)
                v.tensor_tensor(h.rearrange("p (c n) -> p c n", c=2), s1.rearrange("p (c n) -> p c n", c=2),
                                ps[:, 2:4, 0:HH], ALU.mult).then_inc(h_ready, 1)

            def h_out(n):
                gate(dve, h_turned, n + 2)
                gate(dve, y_made, n + 1)
                v.tensor_copy(hT[0:HC].rearrange("p (a c) n -> p a (c n)", a=2), ps[0:HC, 4:6, 0:3 * P]).then_inc(hT_ready, 1)

            def y_out(r, i, n):
                gate(dve, y_made, n + 2)
                gate(dve, yb_written[r], i * 16 + 16 * NE // 2)
                v.tensor_copy(yb[:, r], ps[:, 6, 0:D]).then_inc(y_ready, 1)

            product(0, 0)
            with dve.Fori(0, NT // 2 - 1, 1) as i:
                product(1, 2 * i + 1)
                h_out(2 * i)
                y_out(0, i, 2 * i)
                product(0, 2 * i + 2)
                h_out(2 * i + 1)
                y_out(1, i, 2 * i + 1)
            product(1, NT - 1)
            for n in (NT - 2, NT - 1):
                h_out(n)
                y_out(n % 2, NT // 2 - 1, n)

            def ask(b, r):
                v.tensor_copy(ring_i[:, r, :], pos_i[:, bass.ds(b, 1), :].rearrange("p a k -> p (a k)")).then_inc(comb_ready, 1)

            def combine(b, r, i):
                gate(dve, y_back[r], i * 32 + 32)
                then_in(v.scalar_tensor_tensor(acc_block(b), xg[:, r], gate_p[0][:, bass.ds(b, 1)], acc_block(b), ALU.mult, ALU.add), i, 2, r)
                v.scalar_tensor_tensor(acc_block(b), zs[:, r], gate_p[1][:, bass.ds(b, 1)], acc_block(b), ALU.mult, ALU.add).then_inc(out_ready, 1)

            for r in range(2):
                ask(r, r)
            with dve.Fori(0, LASTB // 2, 1) as i:
                for r in range(2):
                    combine(2 * i + r, r, i)
                    gate(dve, out_ready, 2 * i + (r + 1))
                    ask(2 * i + r + 2, r)
            for r in range(2):
                combine(LASTB + r, r, LASTB // 2)


_OUT = ((N, D), "float32")


def kernel(x, src, dst, L0_gnn_W1, L0_gnn_b1, L0_gnn_W2, L0_gnn_b2, L0_ffn_router_w, L0_ffn_w1, L0_ffn_w2, L0_ffn_w3):
    import concourse.bacc as _bacc
    from concourse.bass_utils import run_bass_kernel_spmd as _run

    def edges(a, fill):
        flat = np.full((E_PAD,), fill, np.int32)
        flat[:E_IN] = np.asarray(a)
        return flat

    def hidden_weights(w):
        w = np.asarray(w)
        padded = np.zeros((NE, HP, D), w.dtype)
        padded[:, :HID] = w
        return np.ascontiguousarray(padded.transpose(2, 0, 1).reshape(D, NE * HP))

    def output_weights(w):
        w = np.asarray(w)
        padded = np.zeros((NE, D, HP), w.dtype)
        padded[:, :, :HID] = w
        return np.ascontiguousarray(padded.transpose(2, 0, 1).reshape(HP, NE * D))

    src_flat, dst_flat = edges(src, 0), edges(dst, N)
    arrays = {
        "x": np.ascontiguousarray(x),
        "src": np.ascontiguousarray(src_flat.reshape(TILES, P).T),
        "dst": np.ascontiguousarray(dst_flat.reshape(TILES, P).T),
        "dst_groups": dst_flat.reshape(GP, GQ * JT * P),
        "W1": np.ascontiguousarray(L0_gnn_W1),
        "b1": np.ascontiguousarray(np.asarray(L0_gnn_b1).reshape(KC, P).T),
        "W2": np.ascontiguousarray(L0_gnn_W2),
        "b2": np.ascontiguousarray(L0_gnn_b2).reshape(1, D),
        "router": np.ascontiguousarray(np.asarray(L0_ffn_router_w).T),
        "w1": hidden_weights(L0_ffn_w1),
        "w3": hidden_weights(L0_ffn_w3),
        "w2": output_weights(L0_ffn_w2),
    }
    nc = _bacc.Bacc("TRN2", target_bir_lowering=False, num_devices=1, dynamic_dma_scratch_size=8192)
    args, ins = {}, {}
    for name, a in arrays.items():
        t = nc.dram_tensor(f"in_{name}", a.shape, mybir.dt.from_np(a.dtype), kind="ExternalInput")
        args[name], ins[f"in_{name}"] = t.ap(), a
    args["out"] = nc.dram_tensor("out_rows", _OUT[0], F32, kind="ExternalOutput").ap()
    build(nc, **args)
    r = _run(nc, [ins], core_ids=[0])
    return r.results[0]["out_rows"]
```

```python
from contextlib import ExitStack

import numpy as np

import concourse.bass as bass
from concourse import mybir

ALU = mybir.AluOpType
ACT = mybir.ActivationFunctionType
AX = mybir.AxisListType.X
F32 = mybir.dt.float32
BF16 = mybir.dt.bfloat16
I32 = mybir.dt.int32

P = 128
N = 6250
D = 256
KC = D // P
NBLK = 50
LASTB = N // P
TAIL = N - LASTB * P
E_IN = 206250
JT = 4
SLOTS = 4
ROUNDS = 101
GROUPS = ROUNDS * SLOTS
TILES = GROUPS * JT
E_PAD = TILES * P
GP, GQ = 101, 4
assert GP * GQ == GROUPS and E_PAD >= E_IN and N < NBLK * P
LO = 64
HI = NBLK * P // LO
CT = 16
COUNTS = TILES // CT
CB = 2
assert COUNTS * CT == TILES and COUNTS >= CB * (NBLK - 2)

NE = 8
HID = 682
HC = 114
NHC = 6
HP = HC * NHC
HH = HP // 2
REGION = NBLK * P
RING = 4
NT = 106
assert NT >= (2 * N + NE * (P - 1)) // P and N + P <= REGION
EPS_LN = 1e-5


def build(nc, x, src, dst, dst_groups, W1, b1, W2, b2, router, w1, w3, w2, out):
    with ExitStack() as ctx:
        def sb(name, shape, dt=F32):
            return ctx.enter_context(nc.sbuf_tensor(name, shape, dt))

        def sem(name):
            return ctx.enter_context(nc.semaphore(name))

        def dram(name, shape, dt=F32):
            return nc.dram_tensor(name, shape, dt, kind="Internal").ap()

        U = [dram("u_layer1", (NBLK * P, D)), dram("u_layer2", (NBLK * P, D))]
        bounds_dram = dram("group_bounds", (GROUPS, 2), I32)
        dis_dram = dram("dis_rows", (NBLK, P))
        lists = dram("expert_lists", (NE * REGION, D))
        y_dram = dram("expert_rows", (NT * P, D))

        acc = sb("acc", [P, NBLK, D])
        late = sb("late", [P, NHC * NE * D])
        at = [0]

        def graph_buf(n, dt=F32):
            v = late[:, at[0]:at[0] + n]
            at[0] += n
            assert at[0] <= NHC * NE * D
            return v if dt == F32 else v.bitcast(dt)

        rows = graph_buf(SLOTS * JT * D).rearrange("p (s j d) -> p s j d", s=SLOTS, j=JT)
        src_t = graph_buf(TILES, I32)
        dst_f = graph_buf(TILES)
        gw = graph_buf(2 * KC * D).rearrange("p (l k n) -> p l k n", l=2, k=KC)
        bounds = graph_buf(2 * GROUPS, I32)[0:1, :]
        first_hot = [graph_buf(JT * P).rearrange("p (j n) -> p j n", j=JT) for _ in range(2)]
        more_hot = graph_buf(JT * P).rearrange("p (j n) -> p j n", j=JT)
        dst_i = rows.rearrange("p s j d -> p (s j d)")[:, 0:TILES].bitcast(I32)
        w13 = sb("w13", [P, 2, KC, NE * HP])
        both = w13.rearrange("p a k n -> p (a k n)")[:, 0:RING * 2 * D].rearrange("p (r k d) -> p r k d", r=RING, k=2)
        cflat = w13.rearrange("p a k n -> p (a k n)")
        cat = [0]

        def count_buf(n, dt=F32):
            v = cflat[:, cat[0]:cat[0] + n]
            cat[0] += n
            return v if dt == F32 else v.bitcast(dt)

        lo_i = count_buf(TILES, I32)
        hi_i = count_buf(TILES, I32)
        lo_b = count_buf(TILES // 2, BF16)
        hi_b = count_buf(TILES // 2, BF16)
        gr_i = count_buf(GQ * JT * P, I32)
        hot_hi = [count_buf(CT * HI // 2, BF16).rearrange("p (n t) -> p n t", t=CT) for _ in range(2)]
        hot_lo = [count_buf(CT * LO // 2, BF16).rearrange("p (n t) -> p n t", t=CT) for _ in range(2)]
        numbers = count_buf(CT * HI // 2, BF16).rearrange("p (n t) -> p n t", t=CT)
        gbi = count_buf(2 * GQ, I32)
        gbo = count_buf(2 * GQ, I32)
        count_row = count_buf(LO)
        dis_hl = count_buf(LO)
        dis_bt = count_buf(P)

        ident = sb("ident", [P, P])
        upper = sb("upper", [P, P])
        ones = sb("ones", [P, P])
        iota = sb("iota", [P, P])
        ones_b = sb("ones_b", [P, P], BF16)
        iota_i = sb("iota_i", [P, P], I32)
        part = sb("part", [P, 1])
        part_int = sb("part_int", [P, 1], I32)
        base = sb("base", [P, NBLK])
        idx_ring = sb("idx_ring", [P, SLOTS, JT], I32)
        b1col = sb("b1col", [P, KC])
        b2row = sb("b2row", [P, D])
        zs = sb("zs", [P, 2, D])
        zT = sb("zT", [P, 2, KC, P])
        dis = sb("dis", [P, NBLK])
        mean = sb("mean", [P, NBLK])
        var = sb("var", [P, NBLK])
        rstd = sb("rstd", [P, NBLK])
        tmp = sb("tmp", [P, NBLK])
        tick = sb("tick", [P, SLOTS])
        rw = sb("rw", [P, KC, NE])
        mask = [sb(f"mask{k}", [P, NBLK, NE]) for k in range(2)]
        red = sb("red", [P, NBLK])
        valid = sb("valid", [P, NBLK])
        gate_p = [sb(f"gate{k}", [P, NBLK]) for k in range(2)]
        pos = sb("pos", [P, NBLK, 2])
        pos_i = sb("pos_i", [P, NBLK, 2], I32)
        ring_i = sb("ring_i", [P, RING, 2], I32)
        ering = sb("ering", [P, 8, NE])
        ering_i = sb("ering_i", [P, 3, NE], I32)
        sched_i = sb("sched_i", [1, 2, NT], I32)
        xg = sb("xg", [P, 2, D])
        xT = zT
        s1 = sb("s1", [P, HP])
        h = sb("h", [P, HP])
        hT = sb("hT", [P, NHC, P])
        yb = sb("yb", [P, 2, D])

        def router_buf(flat):
            return flat[:, 0:NBLK * NE].rearrange("p (b e) -> p b e", e=NE)

        logits = router_buf(s1[:])
        prob = router_buf(h[:])
        work = router_buf(hT.rearrange("p c n -> p (c n)"))
        totals = [router_buf(s1[:]), router_buf(zT.rearrange("p r k n -> p (r k n)"))]
        bn = hT.rearrange("p c n -> p (c n)")[:, 0:6 * NBLK].rearrange("p (b q) -> p b q", q=6)
        outgoing = [zs[:, 0], zs[:, 1], xg[:, 0], xg[:, 1]]
        sched = s1[0:1, 0:5 * NT].rearrange("p (q t) -> p q t", q=5)
        w2s = late.rearrange("p (c n) -> p c n", c=NHC)
        ps = ctx.enter_context(nc.psum_tensor("ps", [P, 8, 512], F32))

        psT = [ps[:, r, 0:KC * P].rearrange("p (k n) -> p k n", k=KC) for r in range(2)]
        psM = [ps[:, 2 + r, 0:D] for r in range(2)]
        psFirst = [ps[:, 4 + q, 0:D] for q in range(2)]
        psMore = ps[:, 6, 0:D]
        psCnt = ps[0:HI, 5, 0:LO]
        psWithin = ps[:, 4, 0:NBLK * NE].rearrange("p (b e) -> p b e", e=NE)
        psTotal = ps[:, 5, 0:NBLK * NE].rearrange("p (b e) -> p b e", e=NE)
        psDis = ps[:, 6, 0:NBLK]

        weights_loaded = sem("weights_loaded")
        edges_loaded = sem("edges_loaded")
        groups_loaded = sem("groups_loaded")
        src_loaded = sem("src_loaded")
        pad_zeroed = sem("pad_zeroed")
        x_loaded = sem("x_loaded")
        iotas_made = sem("iotas_made")
        consts_made = sem("consts_made")
        dve_step = sem("dve_step")
        gate_passed = sem("gate_passed")
        hots_ready = sem("hots_ready")
        hots_counted = sem("hots_counted")
        bounds_made = sem("bounds_made")
        bounds_stored = sem("bounds_stored")
        bounds_loaded = sem("bounds_loaded")
        dis_made = sem("dis_made")
        dis_stored = sem("dis_stored")
        dis_back = sem("dis_back")
        dis_turned = sem("dis_turned")
        dis_ready = sem("dis_ready")
        root_asked = sem("root_asked")
        root_taken = sem("root_taken")
        z_scaled = sem("z_scaled")
        z_turned = sem("z_turned")
        zT_ready = sem("zT_ready")
        z_times_w = sem("z_times_w")
        u_ready = sem("u_ready")
        product_out = sem("product_out")
        u_stored = [sem(f"u_stored{r}") for r in range(2)]
        idx_staged = [sem(f"idx_staged{r}") for r in range(SLOTS)]
        rows_landed = [sem(f"rows_landed{r}") for r in range(SLOTS)]
        slot_free = [sem(f"slot_free{r}") for r in range(SLOTS)]
        first_hot_ready = sem("first_hot_ready")
        first_summed = sem("first_summed")
        first_added = sem("first_added")
        more_hot_ready = sem("more_hot_ready")
        more_summed = sem("more_summed")
        more_added = sem("more_added")
        graph_over = sem("graph_over")
        x_again = [sem(f"x_again{r}") for r in range(2)]
        x_used = sem("x_used")
        w13_loaded = sem("w13_loaded")
        w2_loaded = sem("w2_loaded")
        exp_asked = sem("exp_asked")
        exp_made = sem("exp_made")
        mask_ready = sem("mask_ready")
        ranks_made = sem("ranks_made")
        fill_ready = sem("fill_ready")
        scatter_ready = sem("scatter_ready")
        scattered = [sem(f"scattered{r}") for r in range(RING)]
        sched_ready = sem("sched_ready")
        tile_loaded = [sem(f"tile_loaded{r}") for r in range(2)]
        tile_turned = sem("tile_turned")
        xT_ready = sem("xT_ready")
        gates_made = sem("gates_made")
        hidden_made = sem("hidden_made")
        silu_made = sem("silu_made")
        h_ready = sem("h_ready")
        h_turned = sem("h_turned")
        hT_ready = sem("hT_ready")
        y_made = sem("y_made")
        y_ready = sem("y_ready")
        yb_written = [sem(f"yb_written{r}") for r in range(2)]
        comb_ready = sem("comb_ready")
        y_back = [sem(f"y_back{r}") for r in range(RING)]
        first_gated = sem("first_gated")
        out_ready = sem("out_ready")
        out_stored = [sem(f"out_stored{r}") for r in range(2)]

        def gate(eng, s, value):
            eng.wait_ge(s, value)
            eng.sem_inc(gate_passed, 1)

        def dram_block(t, n_blocks, i, r):
            v = t[0:n_blocks * P, :].rearrange("(i r p) d -> i r p d", r=2, p=P)
            return v[bass.ds(i, 1), r].rearrange("a p d -> (a p) d")

        def acc_block(b):
            return acc[:, bass.ds(b, 1), :].rearrange("p a d -> p (a d)")

        UN = 5

        def load_bounds(eng, regs, k, n_groups):
            eng.load(regs[:2 * n_groups], bounds[0:1, bass.ds(k * (2 * SLOTS), 2 * n_groups)])
            return [tuple(eng.snap(g, min_val=0, max_val=NBLK - 1) for g in regs[2 * q:2 * q + 2]) for q in range(n_groups)]

        block = ctx.enter_context(nc.Block())

        @block.sync
        def _(sp):
            sp.dma_start(dst_i, dst).then_inc(edges_loaded, 16)
            sp.dma_start(gr_i[0:GP, :], dst_groups).then_inc(groups_loaded, 16)
            sp.wait_ge(pad_zeroed, 1)
            sp.dma_start(acc[:, 0:LASTB, :], x[0:LASTB * P, :].rearrange("(b p) d -> p b d", p=P)).then_inc(x_loaded, 16)
            sp.dma_start(acc[0:TAIL, LASTB, :], x[LASTB * P:N, :]).then_inc(x_loaded, 16)
            for k, w in enumerate((W1, W2)):
                sp.dma_start(gw[:, k], w.rearrange("(k p) n -> p k n", p=P)).then_inc(weights_loaded, 16)
            sp.dma_start(b1col[:], b1).then_inc(weights_loaded, 16)
            sp.dma_start(b2row[:], b2.to_broadcast([P, D])).then_inc(weights_loaded, 16)
            sp.dma_start(rw[:], router.rearrange("(k p) e -> p k e", p=P)).then_inc(weights_loaded, 16)
            sp.dma_start(src_t, src).then_inc(src_loaded, 16)
            sp.wait_ge(bounds_made, 1)
            sp.dma_start(bounds_dram.rearrange("(p q) c -> p (q c)", q=GQ), gbo[0:GP, :]).then_inc(bounds_stored, 16)
            sp.wait_ge(bounds_stored, 16)
            sp.dma_start(bounds, bounds_dram.rearrange("(a g) c -> a (g c)", a=1)).then_inc(bounds_loaded, 16)
            sp.wait_ge(dis_made, 1)
            sp.dma_start(dis_dram.rearrange("b (c n) -> (b c) n", n=LO), dis_hl[0:HI, :]).then_inc(dis_stored, 16)
            sp.wait_ge(dis_stored, 16)
            sp.dma_start(dis_bt[0:NBLK, :], dis_dram).then_inc(dis_back, 16)
            for layer in range(2):
                with sp.Fori(0, NBLK // 2, 1) as i:
                    for r in range(2):
                        if layer == 0:
                            sp.wait_ge(u_ready, 2 * i + (r + 1))
                        else:
                            sp.wait_ge(product_out, 2 * i + (NBLK + r + 3))
                        sp.dma_start(dram_block(U[layer], NBLK, i, r), acc_block(2 * i + r)).then_inc(u_stored[r], 16)
                if layer == 0:
                    for a, w in enumerate((w1, w3)):
                        sp.dma_start(w13[:, a], w.rearrange("(k p) n -> p k n", p=P)).then_inc(w13_loaded, 16)
            with sp.Fori(0, LASTB // 2, 1) as i:
                for r in range(2):
                    sp.wait_ge(x_used, 2 * i + (r + 1))
                    sp.dma_start(xg[:, r], dram_block(x, LASTB, i, r)).then_inc(x_again[r], 16)
            sp.wait_ge(x_used, LASTB + 1)
            sp.dma_start(xg[0:TAIL, 0], x[LASTB * P:N, :]).then_inc(x_again[0], 16)
            sp.wait_ge(graph_over, 1)
            sp.dma_start(w2s[0:HC], w2.rearrange("(c p) n -> p c n", p=HC)).then_inc(w2_loaded, 16)
            sp.wait_ge(sched_ready, 1)
            for r in range(RING):
                sp.wait_ge(scattered[r], 32 * (LASTB // RING + (r == 0)))
            for r in range(2):
                sp.wait_ge(yb_written[r], 16 * NE // 2)
            with sp.Fori(0, NT // 2, 1) as i:
                for r in range(2):
                    row = sp.value_load(sched_i[0:1, 1, bass.ds(2 * i + r, 1)], min_val=0, max_val=NE * REGION - P)
                    sp.wait_ge(tile_turned, 2 * i + (r + 1))
                    sp.dma_start(xg[:, r], lists[bass.ds(row, P), :]).then_inc(tile_loaded[r], 16)
            with sp.Fori(0, LASTB // 2, 1) as i:
                for r in range(2):
                    sp.wait_ge(out_ready, 2 * i + (r + 1))
                    sp.dma_start(dram_block(out, LASTB, i, r), acc_block(2 * i + r)).then_inc(out_stored[r], 16)
            sp.wait_ge(out_ready, LASTB + 1)
            sp.dma_start(out[LASTB * P:N, :], acc[0:TAIL, LASTB, :]).then_inc(out_stored[0], 16)
            sp.wait_ge(out_stored[0], 16 * (LASTB // 2 + 1))
            sp.wait_ge(out_stored[1], 16 * (LASTB // 2))

        @block.gpsimd
        def _(pool):
            nc.gpsimd.iota(iota_i[:], pattern=[[1, P]], base=0, channel_multiplier=0).then_inc(iotas_made, 1)
            nc.gpsimd.iota(part_int[:], pattern=[[0, 1]], base=0, channel_multiplier=1).then_inc(iotas_made, 1)
            for layer in range(2):
                for r in range(2):
                    pool.wait_ge(u_stored[r], 16 * (NBLK // 2) * (layer + 1))
                with pool.Fori(0, ROUNDS, 1) as k:
                    for r in range(SLOTS):
                        gate(pool, idx_staged[r], k + (layer * ROUNDS + 1))
                        for j in range(JT):
                            pool.indirect_dma_start(out=rows[:, r, j], out_offset=None, in_=U[layer],
                                                    in_offset=bass.IndirectOffsetOnAxis(ap=idx_ring[:, r, j:j + 1], axis=0)).then_inc(rows_landed[r], 16)
            pool.wait_ge(fill_ready, 1)
            for e in range(NE):
                pool.indirect_dma_start(out=lists, out_offset=bass.IndirectOffsetOnAxis(ap=ering_i[:, 0, e:e + 1], axis=0),
                                        in_=yb[:, e % 2], in_offset=None).then_inc(yb_written[e % 2], 16)
            with pool.Fori(0, LASTB // RING, 1) as i:
                for r in range(RING):
                    gate(pool, scatter_ready, RING * i + (r + 1))
                    for k in range(2):
                        pool.indirect_dma_start(out=lists, out_offset=bass.IndirectOffsetOnAxis(ap=ring_i[:, r, k:k + 1], axis=0),
                                                in_=outgoing[r], in_offset=None).then_inc(scattered[r], 16)
            pool.wait_ge(scatter_ready, LASTB + 1)
            for k in range(2):
                pool.indirect_dma_start(out=lists, out_offset=bass.IndirectOffsetOnAxis(ap=ring_i[0:TAIL, 0, k:k + 1], axis=0),
                                        in_=outgoing[0][0:TAIL], in_offset=None).then_inc(scattered[0], 16)
            with pool.Fori(0, NT // 2, 1) as i:
                for r in range(2):
                    gate(pool, y_ready, 2 * i + (r + 2))
                    pool.dma_start(dram_block(y_dram, NT, i, r), yb[:, r]).then_inc(yb_written[r], 16)
            for r in range(2):
                pool.wait_ge(yb_written[r], 16 * (NT // 2 + NE // 2))
            def gather_both(r, n):
                gate(pool, comb_ready, n + 1)
                for k in range(2):
                    pool.indirect_dma_start(out=both[:, r, k], out_offset=None, in_=y_dram,
                                            in_offset=bass.IndirectOffsetOnAxis(ap=ring_i[:, r, k:k + 1], axis=0)).then_inc(y_back[r], 16)

            with pool.Fori(0, LASTB // RING, 1) as i:
                for r in range(RING):
                    gather_both(r, RING * i + r)
            gather_both(0, LASTB)

        @block.scalar
        def _(act):
            act.sem_inc(xT_ready, 1)

            def root(n, to, of):
                act.wait_ge(root_asked, n)
                nc.scalar.activation(to, of, ACT.Sqrt).then_inc(root_taken, 1)

            root(1, rstd[:], tmp[:])
            act.wait_ge(weights_loaded, 16 * 5)

            def turned(layer, r, n):
                gate(act, z_turned, n + (NBLK * layer + 3))
                if layer == 1:
                    gate(act, z_times_w, n + (NBLK * layer - 1))
                    for k in range(KC):
                        ins = nc.scalar.activation(zT[:, r, k], psT[r][:, k], ACT.Relu, bias=b1col[:, k:k + 1])
                    ins.then_inc(zT_ready, 1)
                else:
                    nc.scalar.copy(zT[:, r], psT[r]).then_inc(zT_ready, 1)

            def product_of(layer, r, n):
                if layer == 1:
                    return
                gate(act, z_times_w, n + (NBLK * layer + 1))
                if layer == 2:
                    nc.scalar.copy(logits[:, bass.ds(n, 1), :].rearrange("p a e -> p (a e)"), psM[r][:, 0:NE]).then_inc(product_out, 1)
                else:
                    nc.scalar.copy(acc_block(n), psM[r]).then_inc(product_out, 1)

            for layer in range(3):
                if layer == 2:
                    root(3, rstd[:], tmp[:])
                    root(4, rstd[:], tmp[:])
                turned(layer, 0, 0)
                with act.Fori(0, NBLK // 2 - 1, 1) as i:
                    for r in range(2):
                        turned(layer, 1 - r, 2 * i + (r + 1))
                        product_of(layer, r, 2 * i + r)
                turned(layer, 1, NBLK - 1)
                for r in range(2):
                    product_of(layer, r, NBLK - 2 + r)
                if layer == 0:
                    root(2, dis_hl[0:HI, :], count_row[0:HI, :])
                    act.wait_ge(src_loaded, 16)
                if layer < 2:
                    with act.Fori(0, ROUNDS, 1) as k:
                        for r in range(SLOTS):
                            gate(act, slot_free[r], k + (layer * ROUNDS + 1))
                            nc.scalar.copy(idx_ring[:, r, :], src_t[:, bass.ds((k * SLOTS + r) * JT, JT)]).then_inc(idx_staged[r], 1)
            act.wait_ge(exp_asked, 1)
            nc.scalar.activation(prob, work, ACT.Exp).then_inc(exp_made, 1)

            def silu(n):
                gate(act, gates_made, n + 1)
                gate(act, h_ready, n + 1)
                nc.scalar.activation(s1.rearrange("p (c n) -> p c n", c=2), ps[:, 0:2, 0:HH], ACT.Silu).then_inc(silu_made, 1)

            def turned_out(r, n):
                gate(act, tile_turned, n + 3)
                nc.scalar.copy(xT[:, r], ps[:, 7, 0:KC * P].rearrange("p (k n) -> p k n", k=KC)).then_inc(xT_ready, 1)

            turned_out(0, 0)
            with act.Fori(0, NT // 2 - 1, 1) as i:
                silu(2 * i)
                turned_out(1, 2 * i + 1)
                silu(2 * i + 1)
                turned_out(0, 2 * i + 2)
            silu(NT - 2)
            turned_out(1, NT - 1)
            silu(NT - 1)

        @block.tensor
        def _(pe):
            pe.sem_inc(hots_counted, 2)
            pe.sem_inc(first_summed, 2)
            pe.sem_inc(more_summed, 1)
            pe.sem_inc(z_turned, 2)
            pe.sem_inc(tile_turned, 2)
            pe.sem_inc(h_turned, 1)
            pe.sem_inc(y_made, 1)
            pe.wait_ge(consts_made, 1)
            nc.tensor.matmul(psCnt, ones_b[0:1, 0:HI], ones_b[0:1, 0:LO], start=True, stop=True, skip_group_check=True)

            def count(r, n):
                pe.wait_ge(hots_ready, n + 1)
                for t in range(CT):
                    mm = nc.tensor.matmul(psCnt, hot_hi[r][:, :, t], hot_lo[r][:, :, t], start=False, stop=True, skip_group_check=True)
                mm.then_inc(hots_counted, 1)

            pe.wait_ge(weights_loaded, 16 * 5)
            steps = pe.alloc_register("pe_steps")
            pe.reg_mov(steps, 0)
            bound_regs = [pe.alloc_register(f"pe_bound{q}") for q in range(2 * SLOTS)]
            for layer in range(3):
                w = (gw[:, 0], gw[:, 1], rw[:])[layer]

                def turn(r, n):
                    pe.wait_ge(z_scaled, n + (NBLK * layer + 1))
                    for k in range(KC):
                        mm = nc.tensor.transpose(psT[r][:, k], zs[:, r, k * P:(k + 1) * P], ident[:])
                    mm.then_inc(z_turned, 1)

                def times_w(r, n):
                    pe.wait_ge(zT_ready, n + (NBLK * layer + 1))
                    pe.wait_ge(product_out, n + (NBLK * layer + 1))
                    for k in range(KC):
                        mm = nc.tensor.matmul(psM[r][:, 0:NE] if layer == 2 else psM[r], zT[:, r, k], w[:, k],
                                              start=k == 0, stop=k == KC - 1)
                    mm.then_inc(z_times_w, 1)

                turn(0, 0)
                with pe.Fori(0, NBLK // 2 - 1, 1) as i:
                    for r in range(2):
                        turn(1 - r, 2 * i + (r + 1))
                        times_w(r, 2 * i + r)
                        if layer == 0:
                            for q in range(CB):
                                count(q, 2 * CB * i + (CB * r + q))
                turn(1, NBLK - 1)
                for r in range(2):
                    times_w(r, NBLK - 2 + r)
                if layer == 0:
                    for n in range(CB * (NBLK - 2), COUNTS):
                        count(n % 2, n)
                    pe.wait_ge(dis_back, 16)
                    nc.tensor.transpose(psDis, dis_bt[0:NBLK, :], ident[0:NBLK, 0:NBLK]).then_inc(dis_turned, 1)
                if layer == 2:
                    break
                pe.wait_ge(bounds_loaded, 16)

                def sum_first(k, r):
                    n = k * SLOTS + (layer * GROUPS + r)
                    pe.wait_ge(rows_landed[r % SLOTS], k * (16 * JT) + 16 * JT * (layer * ROUNDS + 1 + r // SLOTS))
                    pe.wait_ge(first_hot_ready, n + 1)
                    pe.wait_ge(first_added, n + 1)
                    for j in range(JT):
                        mm = nc.tensor.matmul(psFirst[r % 2], first_hot[r % 2][:, j], rows[:, r % SLOTS, j], start=j == 0, stop=j == JT - 1)
                    mm.then_inc(first_summed, 1)

                def sum_more(r, first, last):
                    with pe.If_lt(bound_regs[2 * r], bound_regs[2 * r + 1]):
                        with pe.Fori(first + 1, last + 1, 1):
                            n = pe.snap(steps)
                            pe.wait_ge(more_hot_ready, n + 1)
                            pe.wait_ge(more_added, n + 1)
                            for j in range(JT):
                                mm = nc.tensor.matmul(psMore, more_hot[:, j], rows[:, r, j], start=j == 0, stop=j == JT - 1)
                            mm.then_inc(more_summed, 1)
                            pe.reg_add(steps, steps, 1)

                sum_first(0, 0)
                with pe.Fori(0, ROUNDS - 1, 1) as k:
                    spans = load_bounds(pe, bound_regs, k, SLOTS)
                    for r in range(SLOTS):
                        sum_first(k, r + 1)
                        sum_more(r, *spans[r])
                spans = load_bounds(pe, bound_regs, ROUNDS - 1, SLOTS)
                for r in range(SLOTS):
                    if r + 1 < SLOTS:
                        sum_first(ROUNDS - 1, r + 1)
                    sum_more(r, *spans[r])
            pe.wait_ge(mask_ready, 1)
            flat = work.rearrange("p b e -> p (b e)")
            nc.tensor.matmul(ps[:, 4, 0:NBLK * NE], upper[:], flat, start=True, stop=True)
            nc.tensor.matmul(ps[:, 5, 0:NBLK * NE], ones[:], flat, start=True, stop=True).then_inc(ranks_made, 1)

            def turn_tile(r, i, n):
                pe.wait_ge(tile_loaded[r], i * 16 + 16)
                pe.wait_ge(xT_ready, n + 1)
                for k in range(KC):
                    mm = nc.tensor.transpose(ps[:, 7, k * P:(k + 1) * P], xg[:, r, k * P:(k + 1) * P], ident[:])
                mm.then_inc(tile_turned, 1)

            def hidden(r, n, e):
                pe.wait_ge(xT_ready, n + 2)
                pe.wait_ge(h_ready, n + 1)
                for a in range(2):
                    for c in range(2):
                        for k in range(KC):
                            mm = nc.tensor.matmul(ps[:, 2 * a + c, 0:HH], xT[:, r, k],
                                                  w13[:, a, k, bass.ds(e * HP + c * HH, HH)], start=k == 0, stop=k == KC - 1)
                    mm.then_inc((gates_made, hidden_made)[a], 1)

            def turn_h(n):
                pe.wait_ge(h_ready, n + 2)
                pe.wait_ge(hT_ready, n + 1)
                for c in range(NHC):
                    mm = nc.tensor.transpose(ps[0:HC, 4 + c // 3, (c % 3) * P:(c % 3 + 1) * P], h[:, c * HC:(c + 1) * HC], ident[:])
                mm.then_inc(h_turned, 1)

            def out_rows(n, e):
                pe.wait_ge(hT_ready, n + 2)
                pe.wait_ge(y_ready, n + 1)
                for c in range(NHC):
                    mm = nc.tensor.matmul(ps[:, 6, 0:D], hT[0:HC, c, :], w2s[0:HC, c, bass.ds(e * D, D)], start=c == 0, stop=c == NHC - 1)
                mm.then_inc(y_made, 1)

            pe.wait_ge(sched_ready, 1)
            pe.wait_ge(w13_loaded, 32)
            pe.wait_ge(w2_loaded, 16)
            e_regs = [pe.alloc_register(f"pe_expert{q}") for q in range(4)]

            def load_experts(regs, n):
                pe.load(regs, sched_i[0:1, 0, bass.ds(n, 2)])

            def expert(q):
                return pe.snap(e_regs[q], min_val=0, max_val=NE - 1)

            load_experts(e_regs[0:2], 0)
            turn_tile(0, 0, 0)
            hidden(0, 0, expert(0))
            turn_tile(1, 0, 1)
            hidden(1, 1, expert(1))
            turn_h(0)
            turn_tile(0, 1, 2)
            with pe.Fori(0, NT // 2 - 2, 1) as i:
                load_experts(e_regs[2:4], 2 * i + 2)
                hidden(0, 2 * i + 2, expert(2))
                turn_h(2 * i + 1)
                turn_tile(1, i + 1, 2 * i + 3)
                out_rows(2 * i, expert(0))
                hidden(1, 2 * i + 3, expert(3))
                turn_h(2 * i + 2)
                turn_tile(0, i + 2, 2 * i + 4)
                out_rows(2 * i + 1, expert(1))
                for q in range(2):
                    pe.reg_mov(e_regs[q], e_regs[2 + q])
            load_experts(e_regs[2:4], NT - 2)
            hidden(0, NT - 2, expert(2))
            turn_h(NT - 3)
            turn_tile(1, NT // 2 - 1, NT - 1)
            out_rows(NT - 4, expert(0))
            hidden(1, NT - 1, expert(3))
            turn_h(NT - 2)
            out_rows(NT - 3, expert(1))
            turn_h(NT - 1)
            out_rows(NT - 2, expert(2))
            out_rows(NT - 1, expert(3))

        @block.vector
        def _(dve):
            v = nc.vector
            dve.sem_inc(first_added, 2)
            dve.sem_inc(more_added, 1)
            dve.sem_inc(product_out, 2)
            dve.sem_inc(x_used, 2)
            dve.sem_inc(h_ready, 1)
            dve.sem_inc(hT_ready, 1)
            dve.sem_inc(y_ready, 1)
            for r in range(SLOTS):
                dve.sem_inc(slot_free[r], 1)

            done = [0]

            def then(ins):
                ins.then_inc(dve_step, 1)
                done[0] += 1
                dve.wait_ge(dve_step, done[0])

            v.memset(acc[:, LASTB:NBLK, :], 0.0).then_inc(pad_zeroed, 1)
            v.memset(ones[:], 1.0)
            then(v.memset(ones_b[:], 1.0))
            dve.wait_ge(iotas_made, 2)
            v.tensor_copy(iota[:], iota_i[:])
            then(v.tensor_copy(part[:], part_int[:]))
            v.tensor_scalar(ident[:], iota[:], part[:, 0:1], None, ALU.is_equal)
            v.tensor_scalar(upper[:], iota[:], part[:, 0:1], None, ALU.is_gt)
            v.tensor_copy(numbers, iota[:, 0:HI].unsqueeze(2).to_broadcast([P, HI, CT]))
            then(v.tensor_scalar(base[:], iota[:, 0:NBLK], float(P), None, ALU.mult))
            v.tensor_scalar(valid[:], base[:], part[:, 0:1], float(N), ALU.add, ALU.is_lt).then_inc(consts_made, 1)
            dve.wait_ge(edges_loaded, 16)
            v.tensor_copy(dst_f, dst_i)
            v.tensor_scalar(lo_i, dst_i, LO - 1, None, ALU.bitwise_and)
            then(v.tensor_scalar(hi_i, dst_i, 6, None, ALU.logical_shift_right))
            v.tensor_copy(lo_b, lo_i)
            then(v.tensor_copy(hi_b, hi_i))
            dve.wait_ge(groups_loaded, 16)
            gr = gr_i[0:GP, :].rearrange("p (q e) -> p q e", q=GQ)
            v.tensor_reduce(gbi[0:GP, 0:GQ], gr, AX, ALU.min)
            then(v.tensor_reduce(gbi[0:GP, GQ:2 * GQ], gr, AX, ALU.max))
            then(v.tensor_scalar(gbi[0:GP, :], gbi[0:GP, :], 7, None, ALU.logical_shift_right))
            pair = gbo[0:GP, :].rearrange("p (q c) -> p q c", c=2)
            v.tensor_copy(pair[:, :, 0], gbi[0:GP, 0:GQ])
            v.tensor_copy(pair[:, :, 1], gbi[0:GP, GQ:2 * GQ]).then_inc(bounds_made, 1)

            def moments():
                v.tensor_tensor(mean[:], bn[:, :, 1], bn[:, :, 4], ALU.add)
                v.tensor_tensor(var[:], bn[:, :, 2], bn[:, :, 5], ALU.add)
                then(v.tensor_tensor(tmp[:], bn[:, :, 1], bn[:, :, 4], ALU.subtract))
                v.tensor_scalar(mean[:], mean[:], 0.5, None, ALU.mult)
                then(v.tensor_tensor(tmp[:], tmp[:], tmp[:], ALU.mult))
                then(v.scalar_tensor_tensor(var[:], tmp[:], float(D // 4), var[:], ALU.mult, ALU.add))
                then(v.tensor_scalar(var[:], var[:], 1.0 / D, None, ALU.mult))

            def one_over_std(n):
                v.tensor_scalar(tmp[:], var[:], EPS_LN, None, ALU.add).then_inc(root_asked, 1)
                dve.wait_ge(root_taken, n)
                then(v.reciprocal(rstd[:], rstd[:]))

            dve.wait_ge(x_loaded, 32)
            def stats_of(b):
                return v.bn_stats(bn[:, bass.ds(b, 1), :].rearrange("p a q -> p (a q)"), acc_block(b))

            with dve.Fori(0, NBLK // UN, 1) as i:
                for q in range(UN):
                    stats_of(UN * i + q).then_inc(dve_step, 1)
            done[0] += NBLK
            dve.wait_ge(dve_step, done[0])
            moments()
            one_over_std(1)
            dve.wait_ge(weights_loaded, 16 * 5)
            steps = dve.alloc_register("dve_steps")
            dve.reg_mov(steps, 0)
            bound_regs = [dve.alloc_register(f"dve_bound{q}") for q in range(2 * SLOTS + 2)]
            for layer in range(3):
                if layer == 2:
                    def z_block(b):
                        return v.scalar_tensor_tensor(acc_block(b), acc_block(b), dis[:, bass.ds(b, 1)], b2row[:], ALU.mult, ALU.add)

                    with dve.Fori(0, NBLK // UN, 1) as i:
                        for q in range(UN):
                            z_block(UN * i + q).then_inc(dve_step, 1)
                        for q in range(UN):
                            gate(dve, dve_step, UN * i + (done[0] + q + 1))
                            stats_of(UN * i + q)
                    done[0] += NBLK
                    then(v.memset(tick[:, 0:1], 0.0))
                    moments()
                    then(v.tensor_tensor(tmp[:], mean[:], mean[:], ALU.mult))
                    then(v.tensor_tensor(tmp[:], tmp[:], var[:], ALU.add))
                    v.tensor_scalar(tmp[:], tmp[:], float(D), None, ALU.mult).then_inc(root_asked, 1)
                    dve.wait_ge(root_taken, 3)
                    then(v.tensor_scalar(rstd[:], rstd[:], 1e-12, None, ALU.max))
                    then(v.reciprocal(red[:], rstd[:]))

                    def residual(rows, b, x_rows):
                        return v.scalar_tensor_tensor(rows, rows, red[0:rows.shape[0], bass.ds(b, 1)], x_rows, ALU.mult, ALU.add)

                    with dve.Fori(0, LASTB // 2, 1) as i:
                        for r in range(2):
                            gate(dve, x_again[r], i * 16 + 16)
                            residual(acc_block(2 * i + r), 2 * i + r, xg[:, r]).then_inc(x_used, 1)
                        for r in range(2):
                            gate(dve, x_used, 2 * i + (r + 3))
                            stats_of(2 * i + r)
                    dve.wait_ge(x_again[0], 16 * (LASTB // 2 + 1))
                    then(residual(acc[0:TAIL, LASTB, :], LASTB, xg[0:TAIL, 0]))
                    then(stats_of(LASTB))
                    moments()
                    one_over_std(4)

                def scale(r, n):
                    gate(dve, z_turned, n + (NBLK * layer + 1))
                    if layer == 1:
                        v.tensor_scalar(zs[:, r], acc_block(n), dis[:, bass.ds(n, 1)], None, ALU.mult).then_inc(z_scaled, 1)
                    else:
                        v.tensor_scalar(zs[:, r], acc_block(n), mean[:, bass.ds(n, 1)], rstd[:, bass.ds(n, 1)], ALU.subtract, ALU.mult).then_inc(z_scaled, 1)

                def count(r, n):
                    gate(dve, hots_counted, n + 1)
                    v.tensor_tensor(hot_hi[r], hi_b[:, bass.ds(n * CT, CT)].unsqueeze(1).to_broadcast([P, HI, CT]), numbers, ALU.is_equal)
                    v.tensor_tensor(hot_lo[r], lo_b[:, bass.ds(n * CT, CT)].unsqueeze(1).to_broadcast([P, LO, CT]), numbers[:, 0:LO], ALU.is_equal).then_inc(hots_ready, 1)

                def times_dis(r, n):
                    gate(dve, z_times_w, n + (NBLK * layer + 1))
                    v.tensor_scalar(acc_block(n), psM[r], dis[:, bass.ds(n, 1)], None, ALU.mult).then_inc(product_out, 1)

                for r in range(2):
                    scale(r, r)
                with dve.Fori(0, NBLK // 2 - 1, 1) as i:
                    for r in range(2):
                        if layer == 0:
                            for q in range(CB):
                                count(q, 2 * CB * i + (CB * r + q))
                        scale(r, 2 * i + (r + 2))
                        if layer == 1:
                            times_dis(r, 2 * i + r)
                if layer == 1:
                    for r in range(2):
                        times_dis(r, NBLK - 2 + r)
                if layer == 0:
                    for n in range(CB * (NBLK - 2), COUNTS):
                        count(n % 2, n)
                    dve.wait_ge(hots_counted, 2 + COUNTS)
                    v.tensor_copy(count_row[0:HI, :], psCnt).then_inc(root_asked, 1)
                    dve.wait_ge(root_taken, 2)
                    v.reciprocal(dis_hl[0:HI, :], dis_hl[0:HI, :]).then_inc(dis_made, 1)
                    dve.wait_ge(dis_turned, 1)
                    then(v.tensor_copy(dis[:], psDis))
                    dve.wait_ge(product_out, 2 + NBLK)
                    with dve.Fori(0, NBLK // UN, 1) as i:
                        for q in range(UN):
                            b = UN * i + q
                            v.tensor_scalar(acc_block(b), acc_block(b), dis[:, bass.ds(b, 1)], None, ALU.mult).then_inc(u_ready, 1)
                if layer == 2:
                    break
                dve.wait_ge(bounds_loaded, 16)

                def hots(to, k, r, b):
                    for j in range(JT):
                        ins = v.tensor_scalar(to[:, j], iota[:], base[:, bass.ds(b, 1)],
                                              dst_f[:, bass.ds(k * (SLOTS * JT) + (r * JT + j), 1)], ALU.add, ALU.is_equal)
                    return ins

                def first_hots(k, r, b):
                    gate(dve, first_summed, k * SLOTS + (layer * GROUPS + r + 1))
                    hots(first_hot[r % 2], k, r, b).then_inc(first_hot_ready, 1)

                def add_sums(k, r, first, last):
                    n = k * SLOTS + (layer * GROUPS + r)
                    gate(dve, first_summed, n + 3)
                    gate(dve, first_added, n + 2)
                    v.tensor_tensor(acc_block(first), acc_block(first), psFirst[r % 2], ALU.add).then_inc(first_added, 1)
                    with dve.If_lt(bound_regs[2 * r], bound_regs[2 * r + 1]):
                        with dve.Fori(first + 1, last + 1, 1) as b:
                            m = dve.snap(steps)
                            hots(more_hot, k, r, b).then_inc(more_hot_ready, 1)
                            gate(dve, more_summed, m + 2)
                            v.tensor_tensor(acc_block(b), acc_block(b), psMore, ALU.add).then_inc(more_added, 1)
                            gate(dve, more_added, m + 2)
                            dve.reg_add(steps, steps, 1)
                    v.memset(tick[:, r:r + 1], 0.0).then_inc(slot_free[r], 1)

                spans = load_bounds(dve, bound_regs, 0, 1)
                first_hots(0, 0, spans[0][0])
                with dve.Fori(0, ROUNDS - 1, 1) as k:
                    spans = load_bounds(dve, bound_regs, k, SLOTS + 1)
                    for r in range(SLOTS):
                        first_hots(k, r + 1, spans[r + 1][0])
                        add_sums(k, r, *spans[r])
                spans = load_bounds(dve, bound_regs, ROUNDS - 1, SLOTS)
                for r in range(SLOTS):
                    if r + 1 < SLOTS:
                        first_hots(ROUNDS - 1, r + 1, spans[r + 1][0])
                    add_sums(ROUNDS - 1, r, *spans[r])
                dve.wait_ge(first_added, 2 + GROUPS * (layer + 1))
                if layer == 1:
                    v.memset(tick[:, 0:1], 0.0).then_inc(graph_over, 1)

            dve.wait_ge(product_out, 2 + 3 * NBLK)

            def by_token(t):
                return t.unsqueeze(2).to_broadcast([P, NBLK, NE])

            def by_expert(t):
                return t.unsqueeze(1).to_broadcast([P, NBLK, NE])

            e_iota = by_expert(iota[:, 0:NE])
            then(v.tensor_reduce(red[:], logits, AX, ALU.max))
            v.tensor_tensor(work, logits, by_token(red[:]), ALU.subtract).then_inc(exp_asked, 1)
            dve.wait_ge(exp_made, 1)
            then(v.tensor_reduce(red[:], prob, AX, ALU.add))
            then(v.reciprocal(red[:], red[:]))
            then(v.tensor_tensor(prob, prob, by_token(red[:]), ALU.mult))
            for k in range(2):
                then(v.tensor_reduce(gate_p[k][:], prob, AX, ALU.max))
                then(v.tensor_tensor(work, prob, by_token(gate_p[k][:]), ALU.is_equal))
                then(v.scalar_tensor_tensor(work, work, float(-NE), e_iota, ALU.mult, ALU.add))
                then(v.tensor_reduce(red[:], work, AX, ALU.min))
                then(v.tensor_tensor(mask[k][:], work, by_token(red[:]), ALU.is_equal))
                if k == 0:
                    then(v.scalar_tensor_tensor(prob, mask[0][:], -2.0, prob, ALU.mult, ALU.add))
            then(v.tensor_tensor(red[:], gate_p[0][:], gate_p[1][:], ALU.add))
            then(v.tensor_scalar(red[:], red[:], 1e-9, None, ALU.add))
            then(v.reciprocal(red[:], red[:]))
            for k in range(2):
                v.tensor_tensor(gate_p[k][:], gate_p[k][:], red[:], ALU.mult)
                then(v.tensor_tensor(mask[k][:], mask[k][:], by_token(valid[:]), ALU.mult))
            v.tensor_tensor(work, mask[0][:], mask[1][:], ALU.add).then_inc(mask_ready, 1)
            v.memset(yb[:], 0.0)
            dve.wait_ge(ranks_made, 1)
            then(v.tensor_copy(totals[0][:], psTotal))
            cur, reach = 0, 1
            while reach < NBLK:
                v.tensor_copy(totals[1 - cur][:, 0:reach], totals[cur][:, 0:reach])
                then(v.tensor_tensor(totals[1 - cur][:, reach:], totals[cur][:, reach:], totals[cur][:, :NBLK - reach], ALU.add))
                cur, reach = 1 - cur, 2 * reach
            scan = totals[cur]
            count = scan[:, NBLK - 1, :]
            first_row = ering[:, 0, :]
            then(v.tensor_scalar(first_row, iota[:, 0:NE], float(REGION), None, ALU.mult))
            then(v.tensor_tensor(ering[:, 1, :], count, first_row, ALU.add))
            v.tensor_scalar(ering_i[:, 0, :], ering[:, 1, :], part[:, 0:1], None, ALU.add).then_inc(fill_ready, 1)
            then(v.tensor_tensor(work, psWithin, scan, ALU.add))
            then(v.tensor_tensor(work, work, psTotal, ALU.subtract))
            then(v.tensor_tensor(work, work, by_expert(first_row), ALU.add))
            for k in range(2):
                then(v.tensor_tensor(prob, mask[k][:], work, ALU.mult))
                then(v.tensor_reduce(pos[:, :, k], prob, AX, ALU.add))
            then(v.tensor_copy(pos_i[:], pos[:]))

            def for_scatter(b, r):
                v.tensor_scalar(outgoing[r], acc_block(b), mean[:, bass.ds(b, 1)], rstd[:, bass.ds(b, 1)], ALU.subtract, ALU.mult)
                v.tensor_copy(ring_i[:, r, :], pos_i[:, bass.ds(b, 1), :].rearrange("p a k -> p (a k)")).then_inc(scatter_ready, 1)

            for r in range(RING):
                for_scatter(r, r)
            with dve.Fori(1, LASTB // RING, 1) as i:
                for r in range(RING):
                    gate(dve, scattered[r], i * 32)
                    for_scatter(RING * i + r, r)
            dve.wait_ge(scattered[0], 32 * (LASTB // RING))
            for_scatter(LASTB, 0)

            tiles, ends, shift = ering[:, 2, :], ering[:, 3, :], ering[:, 4, :]
            then(v.tensor_scalar(ering_i[:, 1, :], count, float(P - 1), None, ALU.add))
            then(v.tensor_scalar(ering_i[:, 2, :], ering_i[:, 1, :], 7, None, ALU.logical_shift_right))
            then(v.tensor_copy(tiles, ering_i[:, 2, :]))
            then(v.tensor_copy(ends, tiles))
            for e in range(1, NE):
                then(v.tensor_tensor(ends[:, e:e + 1], ends[:, e - 1:e], tiles[:, e:e + 1], ALU.add))
            tile_no, expert, rel, flag, taken = (sched[:, q, :] for q in range(5))
            then(v.tensor_scalar(taken[:, 0:1], ends[0:1, NE - 1:NE], -1.0, None, ALU.add))
            then(v.tensor_scalar(tile_no, iota[0:1, 0:NT], taken[:, 0:1], None, ALU.min))
            v.tensor_copy(rel, tile_no)
            then(v.memset(expert, 0.0))
            for e in range(NE - 1):
                v.tensor_scalar(flag, tile_no, ends[0:1, e:e + 1], None, ALU.is_ge)
                then(v.tensor_scalar(taken, tile_no, ends[0:1, e:e + 1], tiles[0:1, e:e + 1], ALU.is_ge, ALU.mult))
                v.tensor_tensor(expert, expert, flag, ALU.add)
                then(v.tensor_tensor(rel, rel, taken, ALU.subtract))
            v.tensor_copy(sched_i[:, 0, :], expert)
            then(v.tensor_scalar(rel, rel, float(P), None, ALU.mult))
            then(v.scalar_tensor_tensor(flag, expert, float(REGION), rel, ALU.mult, ALU.add))
            v.tensor_copy(sched_i[:, 1, :], flag).then_inc(sched_ready, 1)
            then(v.tensor_tensor(shift, ends, tiles, ALU.subtract))
            then(v.scalar_tensor_tensor(shift, shift, float(P), first_row, ALU.mult, ALU.subtract))
            for k in range(2):
                then(v.tensor_tensor(prob, mask[k][:], by_expert(shift), ALU.mult))
                then(v.tensor_reduce(red[:], prob, AX, ALU.add))
                then(v.tensor_tensor(pos[:, :, k], pos[:, :, k], red[:], ALU.add))
            then(v.tensor_copy(pos_i[:], pos[:]))

            def product(n):
                gate(dve, hidden_made, n + 1)
                gate(dve, silu_made, n + 1)
                gate(dve, h_turned, n + 1)
                v.tensor_tensor(h.rearrange("p (c n) -> p c n", c=2), s1.rearrange("p (c n) -> p c n", c=2),
                                ps[:, 2:4, 0:HH], ALU.mult).then_inc(h_ready, 1)

            def h_out(n):
                gate(dve, h_turned, n + 2)
                gate(dve, y_made, n + 1)
                v.tensor_copy(hT[0:HC].rearrange("p (a c) n -> p a (c n)", a=2), ps[0:HC, 4:6, 0:3 * P]).then_inc(hT_ready, 1)

            def y_out(r, i, n):
                gate(dve, y_made, n + 2)
                gate(dve, yb_written[r], i * 16 + 16 * NE // 2)
                v.tensor_copy(yb[:, r], ps[:, 6, 0:D]).then_inc(y_ready, 1)

            product(0)
            product(1)
            h_out(0)
            with dve.Fori(0, NT // 2 - 1, 1) as i:
                for r in range(2):
                    product(2 * i + (r + 2))
                    h_out(2 * i + (r + 1))
                    y_out(r, i, 2 * i + r)
            h_out(NT - 1)
            for n in (NT - 2, NT - 1):
                y_out(n % 2, NT // 2 - 1, n)

            def ask(b, r):
                v.tensor_copy(ring_i[:, r, :], pos_i[:, bass.ds(b, 1), :].rearrange("p a k -> p (a k)")).then_inc(comb_ready, 1)

            def combine(b, r, i):
                gate(dve, y_back[r], i * 32 + 32)
                v.scalar_tensor_tensor(acc_block(b), both[:, r, 0], gate_p[0][:, bass.ds(b, 1)], acc_block(b), ALU.mult, ALU.add).then_inc(first_gated, 1)
                gate(dve, first_gated, b + 1)
                v.scalar_tensor_tensor(acc_block(b), both[:, r, 1], gate_p[1][:, bass.ds(b, 1)], acc_block(b), ALU.mult, ALU.add).then_inc(out_ready, 1)

            for r in range(RING):
                ask(r, r)
            with dve.Fori(0, LASTB // RING - 1, 1) as i:
                for r in range(RING):
                    combine(RING * i + r, r, i)
                    gate(dve, out_ready, RING * i + (r + 1))
                    ask(RING * i + (r + RING), r)
            for r in range(RING):
                combine(LASTB - RING + r, r, LASTB // RING - 1)
                if r == 0:
                    dve.wait_ge(out_ready, LASTB - RING + 1)
                    ask(LASTB, 0)
            combine(LASTB, 0, LASTB // RING)


_OUT = ((N, D), "float32")


def kernel(x, src, dst, L0_gnn_W1, L0_gnn_b1, L0_gnn_W2, L0_gnn_b2, L0_ffn_router_w, L0_ffn_w1, L0_ffn_w2, L0_ffn_w3):
    import concourse.bacc as _bacc
    from concourse.bass_utils import run_bass_kernel_spmd as _run

    def edges(a, fill):
        flat = np.full((E_PAD,), fill, np.int32)
        flat[:E_IN] = np.asarray(a)
        return flat

    def hidden_weights(w):
        w = np.asarray(w)
        padded = np.zeros((NE, HP, D), w.dtype)
        padded[:, :HID] = w
        return np.ascontiguousarray(padded.transpose(2, 0, 1).reshape(D, NE * HP))

    def output_weights(w):
        w = np.asarray(w)
        padded = np.zeros((NE, D, HP), w.dtype)
        padded[:, :, :HID] = w
        return np.ascontiguousarray(padded.transpose(2, 0, 1).reshape(HP, NE * D))

    src_flat, dst_flat = edges(src, 0), edges(dst, N)
    arrays = {
        "x": np.ascontiguousarray(x),
        "src": np.ascontiguousarray(src_flat.reshape(TILES, P).T),
        "dst": np.ascontiguousarray(dst_flat.reshape(TILES, P).T),
        "dst_groups": dst_flat.reshape(GP, GQ * JT * P),
        "W1": np.ascontiguousarray(L0_gnn_W1),
        "b1": np.ascontiguousarray(np.asarray(L0_gnn_b1).reshape(KC, P).T),
        "W2": np.ascontiguousarray(L0_gnn_W2),
        "b2": np.ascontiguousarray(L0_gnn_b2).reshape(1, D),
        "router": np.ascontiguousarray(np.asarray(L0_ffn_router_w).T),
        "w1": hidden_weights(L0_ffn_w1),
        "w3": hidden_weights(L0_ffn_w3),
        "w2": output_weights(L0_ffn_w2),
    }
    nc = _bacc.Bacc("TRN2", target_bir_lowering=False, num_devices=1, dynamic_dma_scratch_size=8192)
    args, ins = {}, {}
    for name, a in arrays.items():
        t = nc.dram_tensor(f"in_{name}", a.shape, mybir.dt.from_np(a.dtype), kind="ExternalInput")
        args[name], ins[f"in_{name}"] = t.ap(), a
    args["out"] = nc.dram_tensor("out_rows", _OUT[0], F32, kind="ExternalOutput").ap()
    build(nc, **args)
    r = _run(nc, [ins], core_ids=[0])
    return r.results[0]["out_rows"]
```

```python
from contextlib import ExitStack

import numpy as np

import concourse.bass as bass
from concourse import mybir

ALU = mybir.AluOpType
ACT = mybir.ActivationFunctionType
AX = mybir.AxisListType.X
F32 = mybir.dt.float32
BF16 = mybir.dt.bfloat16
F16 = mybir.dt.float16
I32 = mybir.dt.int32

P = 128
N = 6250
D = 256
KC = D // P
NBLK = 50
LASTB = N // P
TAIL = N - LASTB * P
E_IN = 206250
JT = 4
SLOTS = 4
ROUNDS = 101
GROUPS = ROUNDS * SLOTS
TILES = GROUPS * JT
E_PAD = TILES * P
GT = 8
SPANS = TILES // GT
STEP = 8
TURNS = (SPANS - 2) // STEP
assert TURNS * STEP + 2 == SPANS and STEP % 2 == 0
PAIR = GT // JT
GP, GQ = 101, 2
NB = LASTB + 1
assert NB % 2 == 1
assert GP * GQ == SPANS and SLOTS % PAIR == 0 and E_PAD >= E_IN and N < NBLK * P
LO = 64
HI = NBLK * P // LO
CT = 16
COUNTS = TILES // CT
CB = 2
assert COUNTS * CT == TILES and COUNTS >= CB * (NBLK - 2)

CODE = 64
SC = NBLK + 1
CELLS = 10
PARTS = 2
BATCHES = NBLK // CELLS
assert BATCHES * CELLS == NBLK and BATCHES % 2 == 1 and NBLK < CODE - 1

NE = 8
HID = 682
HC = 114
NHC = 6
HP = HC * NHC
HH = HP // 2
REGION = NBLK * P
RING = 4
NT = 106
assert NT >= (2 * N + NE * (P - 1)) // P and N + P <= REGION
EPS_LN = 1e-5
UN, XU = 5, 6


def build(nc, x, src, dst, dst_spans, W1, b1, W2, b2, router, w1, w3, w2, out):
    with ExitStack() as ctx:
        def sb(name, shape, dt=F32):
            return ctx.enter_context(nc.sbuf_tensor(name, shape, dt))

        def sem(name):
            return ctx.enter_context(nc.semaphore(name))

        def dram(name, shape, dt=F32):
            return nc.dram_tensor(name, shape, dt, kind="Internal").ap()

        U = [dram(f"u_layer{k + 1}", (NBLK * P, PARTS * D), F16) for k in range(2)]
        bounds_dram = dram("span_bounds", (SPANS, 2), I32)
        dis_dram = dram("dis_rows", (NBLK, P))
        lists = dram("expert_lists", (NE * REGION, D))
        y_dram = dram("expert_rows", (NT * P, D))

        acc = sb("acc", [P, NBLK, D])
        late = sb("late", [P, NHC * NE * D])
        at = [0]

        def graph_buf(n, dt=F32):
            v = late[:, at[0]:at[0] + n]
            at[0] += n
            assert at[0] <= NHC * NE * D
            return v if dt == F32 else v.bitcast(dt)

        src_t = graph_buf(TILES, I32)
        dst_f = graph_buf(TILES)
        gw = graph_buf(2 * KC * D).rearrange("p (l k n) -> p l k n", l=2, k=KC)
        bounds = graph_buf(2 * SPANS, I32)[0:1, :]
        slots = graph_buf(NBLK * NBLK, BF16).rearrange("p (b q s) -> p b q s", b=NBLK, q=2)
        loops = graph_buf(NBLK)
        scaled_loops = graph_buf(NBLK)
        top_row = graph_buf(P)[0:1, :]
        row_scale = graph_buf(NBLK)
        shared = graph_buf(SLOTS * JT * D)
        rows = shared.bitcast(F16).rearrange("p (s j d) -> p s j d", s=SLOTS, j=JT)
        hot_cols = CELLS * P // 2
        cell_hot = [[shared[:, (2 * r + q) * hot_cols:(2 * r + q + 1) * hot_cols].bitcast(BF16).rearrange("p (n t) -> p n t", t=CELLS)
                     for q in range(2)] for r in range(2)]
        cells = [shared[:, (4 + r) * hot_cols:(5 + r) * hot_cols].bitcast(F16).rearrange("p (t n) -> p t n", t=CELLS) for r in range(2)]
        w13 = sb("w13", [P, 2, KC, NE * HP])
        both = w13.rearrange("p a k n -> p (a k n)")[:, 0:RING * 2 * D].rearrange("p (r k d) -> p r k d", r=RING, k=2)
        cflat = w13.rearrange("p a k n -> p (a k n)")
        W_COLS = 2 * KC * NE * HP
        cat = [0]

        def count_buf(n, dt=F32):
            v = cflat[:, cat[0]:cat[0] + n]
            cat[0] += n
            assert cat[0] <= W_COLS - hot_cols
            return v if dt == F32 else v.bitcast(dt)

        x_rows = cflat[:, 0:NBLK * D].rearrange("p (b d) -> p b d", b=NBLK)
        numbers1 = cflat[:, W_COLS - hot_cols:].bitcast(BF16).rearrange("p (n t) -> p n t", t=CELLS)
        parts = cflat[:, 0:PARTS * NBLK * D // 2].bitcast(F16).rearrange("p (q b d) -> p q b d", q=PARTS, b=NBLK)
        behind = PARTS * NBLK * D // 2
        more_cols = JT * P // 2
        assert behind + 3 * more_cols <= W_COLS - hot_cols
        first_hot = [cflat[:, behind + r * more_cols:behind + (r + 1) * more_cols].bitcast(F16).rearrange("p (j n) -> p j n", j=JT) for r in range(2)]
        more_hot = cflat[:, behind + 2 * more_cols:behind + 3 * more_cols].bitcast(F16).rearrange("p (j n) -> p j n", j=JT)


        lo_i = count_buf(TILES, I32)
        hi_i = count_buf(TILES, I32)
        dst_i = count_buf(TILES, I32)
        lo_b = count_buf(TILES // 2, BF16)
        hi_b = count_buf(TILES // 2, BF16)
        gr_i = count_buf(GQ * GT * P, I32)
        hot_flat = count_buf(CT * (HI + LO))
        hot_hi = [hot_flat[:, r * (CT * HI // 2):(r + 1) * (CT * HI // 2)].bitcast(BF16).rearrange("p (n t) -> p n t", t=CT) for r in range(2)]
        hot_lo = [hot_flat[:, CT * HI + r * (CT * LO // 2):CT * HI + (r + 1) * (CT * LO // 2)].bitcast(BF16).rearrange("p (n t) -> p n t", t=CT)
                  for r in range(2)]
        numbers = count_buf(CT * HI // 2, BF16).rearrange("p (n t) -> p n t", t=CT)
        gbi = count_buf(2 * GQ, I32)
        gbo = count_buf(2 * GQ, I32)
        count_row = count_buf(LO)
        dis_hl = count_buf(LO)
        dis_bt = count_buf(P)
        upper_b = count_buf(P // 2, BF16)
        code = count_buf(TILES)
        src1 = count_buf(TILES // 2, BF16)
        dst1 = count_buf(TILES // 2, BF16)
        rank1 = count_buf(TILES // 2, BF16)
        filled = count_buf(NBLK * SC // 2, BF16).rearrange("p (b s) -> p b s", b=NBLK)[0:1]

        def span_bufs(flat):
            at = [0]

            def take(n):
                at[0] += n
                return flat[:, at[0] - n:at[0]]

            return (take(GT // 2).bitcast(BF16),
                    take(SC * GT // 2).bitcast(BF16).rearrange("p (s t) -> p s t", t=GT),
                    take(GT * NBLK).rearrange("p (t s) -> p t s", t=GT),
                    take(GT),
                    take(SC * GT).bitcast(BF16).rearrange("p (q s t) -> p q s t", q=2, t=GT),
                    take(P * GT // 2).bitcast(BF16).rearrange("p (n t) -> p n t", t=GT))

        first_bufs = [span_bufs(hot_flat), span_bufs(gr_i.bitcast(F32))]
        more_bufs = span_bufs(count_buf(GT // 2 + SC * GT // 2 + GT * NBLK + GT + SC * GT + P * GT // 2))

        ident = sb("ident", [P, P])
        upper = sb("upper", [P, P])
        ones = sb("ones", [P, P])
        iota = sb("iota", [P, P])
        ones_b = sb("ones_b", [P, P], BF16)
        iota_i = sb("iota_i", [P, P], I32)
        part = sb("part", [P, 1])
        part_int = sb("part_int", [P, 1], I32)
        base = sb("base", [P, NBLK])
        base_code = sb("base_code", [P, NBLK])
        left_i = sb("left_i", [P, 1], I32)
        left_col = sb("left_col", [P, 1])
        dis_unscaled = sb("dis_unscaled", [P, NBLK])
        idx_ring = sb("idx_ring", [P, SLOTS, JT], I32)
        b1col = sb("b1col", [P, KC])
        b2row = sb("b2row", [P, D])
        zs = sb("zs", [P, 2, D])
        zT = sb("zT", [P, 2, KC, P])
        dis = sb("dis", [P, NBLK])
        mean = sb("mean", [P, NBLK])
        var = sb("var", [P, NBLK])
        rstd = sb("rstd", [P, NBLK])
        tmp = sb("tmp", [P, NBLK])
        tick = sb("tick", [P, SLOTS])
        rw = sb("rw", [P, KC, NE])
        mask = [sb(f"mask{k}", [P, NBLK, NE]) for k in range(2)]
        red = sb("red", [P, NBLK])
        valid = sb("valid", [P, NBLK])
        gate_p = [sb(f"gate{k}", [P, NBLK]) for k in range(2)]
        pos = sb("pos", [P, NBLK, 2])
        pos_i = sb("pos_i", [P, NBLK, 2], I32)
        ring_i = sb("ring_i", [P, RING, 2], I32)
        ering = sb("ering", [P, 8, NE])
        ering_i = sb("ering_i", [P, 3, NE], I32)
        sched_i = sb("sched_i", [1, 2, NT], I32)
        xg = sb("xg", [P, 2, D])
        xT = zT
        s1 = sb("s1", [P, HP])
        h = sb("h", [P, HP])
        hT = sb("hT", [P, NHC, P])
        yb = sb("yb", [P, 2, D])

        def router_buf(flat):
            return flat[:, 0:NBLK * NE].rearrange("p (b e) -> p b e", e=NE)

        logits = router_buf(s1[:])
        prob = router_buf(h[:])
        work = router_buf(hT.rearrange("p c n -> p (c n)"))
        totals = [router_buf(s1[:]), router_buf(zT.rearrange("p r k n -> p (r k n)"))]
        bn = hT.rearrange("p c n -> p (c n)")[:, 0:6 * NBLK].rearrange("p (b q) -> p b q", q=6)
        outgoing = [zs[:, 0], zs[:, 1], xg[:, 0], xg[:, 1]]
        sched = s1[0:1, 0:5 * NT].rearrange("p (q t) -> p q t", q=5)
        w2s = late.rearrange("p (c n) -> p c n", c=NHC)
        ps = ctx.enter_context(nc.psum_tensor("ps", [P, 8, 512], F32))

        psT = [ps[:, r, 0:KC * P].rearrange("p (k n) -> p k n", k=KC) for r in range(2)]
        psM = [ps[:, 2 + r, 0:D] for r in range(2)]
        psFirst = [ps[:, 4 + q, 0:D] for q in range(2)]
        psMore = ps[:, 6, 0:D]
        psCnt = ps[0:HI, 5, 0:LO]
        psWithin = ps[:, 4, 0:NBLK * NE].rearrange("p (b e) -> p b e", e=NE)
        psTotal = ps[:, 5, 0:NBLK * NE].rearrange("p (b e) -> p b e", e=NE)
        psDis = ps[:, 6, 0:NBLK]

        def prefix_bank(b):
            return ps[:, b, 0:(GT + 1) * SC].rearrange("p (j s) -> p j s", s=SC)

        def slot_bank(b):
            return ps[:, b, 0:2 * SC].rearrange("p (q s) -> p q s", q=2)

        psPrefix, psSlot = [prefix_bank(r) for r in range(2)], [slot_bank(2 + r) for r in range(2)]
        psMorePrefix, psMoreSlot = prefix_bank(4), slot_bank(7)
        psLeft = ps[:, 5, 0:1]
        psTop = ps[0:1, 7, 0:P]
        psScale = ps[:, 6, 0:1]
        psSum = [ps[:, 6 + r, 0:D] for r in range(2)]

        def ps_cell(r, c):
            return ps[:, 3 * r + c // 4, (c % 4) * P:(c % 4 + 1) * P]

        weights_loaded = sem("weights_loaded")
        edges_loaded = sem("edges_loaded")
        spans_loaded = sem("spans_loaded")
        src_loaded = sem("src_loaded")
        pad_zeroed = sem("pad_zeroed")
        x_loaded = sem("x_loaded")
        iotas_made = sem("iotas_made")
        consts_made = sem("consts_made")
        dve_step = sem("dve_step")
        gate_passed = sem("gate_passed")
        hots_ready = sem("hots_ready")
        hots_counted = sem("hots_counted")
        bounds_made = sem("bounds_made")
        bounds_stored = sem("bounds_stored")
        bounds_loaded = sem("bounds_loaded")
        dis_made = sem("dis_made")
        dis_stored = sem("dis_stored")
        dis_back = sem("dis_back")
        dis_turned = sem("dis_turned")
        dis_ready = sem("dis_ready")
        root_asked = sem("root_asked")
        root_taken = sem("root_taken")
        z_scaled = sem("z_scaled")
        z_turned = sem("z_turned")
        zT_ready = sem("zT_ready")
        z_times_w = sem("z_times_w")
        product_out = sem("product_out")
        u_stored = [sem(f"u_stored{r}") for r in range(2)]
        idx_staged = [sem(f"idx_staged{r}") for r in range(SLOTS)]
        rows_landed = [sem(f"rows_landed{r}") for r in range(SLOTS)]
        slot_free = [sem(f"slot_free{r}") for r in range(SLOTS)]
        first_hot_ready = sem("first_hot_ready")
        first_summed = sem("first_summed")
        first_added = sem("first_added")
        more_hot_ready = sem("more_hot_ready")
        more_summed = sem("more_summed")
        more_added = sem("more_added")
        graph_over = sem("graph_over")
        marks_made = sem("marks_made")
        prefix_made = sem("prefix_made")
        filled_kept = sem("filled_kept")
        slot_hots_made = sem("slot_hots_made")
        slots_summed = sem("slots_summed")
        slots_added = sem("slots_added")
        bucket_step = sem("bucket_step")
        more_marks_made = sem("more_marks_made")
        more_prefix_made = sem("more_prefix_made")
        more_filled_kept = sem("more_filled_kept")
        more_slot_hots_made = sem("more_slot_hots_made")
        more_slots_summed = sem("more_slots_summed")
        more_step = sem("more_step")
        left_asked = sem("left_asked")
        left_summed = sem("left_summed")
        left_known = sem("left_known")
        high_made = sem("high_made")
        tops_made = sem("tops_made")
        tops_turned = sem("tops_turned")
        top_made = sem("top_made")
        top_spread = sem("top_spread")
        scale_made = sem("scale_made")
        parts_made = sem("parts_made")
        cell_hots_made = sem("cell_hots_made")
        cells_counted = sem("cells_counted")
        cells_ready = sem("cells_ready")
        cells_used = sem("cells_used")
        sums_taken = sem("sums_taken")
        x_again = sem("x_again")
        x_used = sem("x_used")
        z_made = sem("z_made")
        squares_summed = sem("squares_summed")
        w13_loaded = sem("w13_loaded")
        w2_loaded = sem("w2_loaded")
        exp_asked = sem("exp_asked")
        exp_made = sem("exp_made")
        mask_ready = sem("mask_ready")
        ranks_made = sem("ranks_made")
        fill_ready = sem("fill_ready")
        scatter_ready = sem("scatter_ready")
        scattered = [sem(f"scattered{r}") for r in range(RING)]
        sched_ready = sem("sched_ready")
        tile_loaded = [sem(f"tile_loaded{r}") for r in range(2)]
        tile_turned = sem("tile_turned")
        xT_ready = sem("xT_ready")
        gates_made = sem("gates_made")
        hidden_made = sem("hidden_made")
        silu_made = sem("silu_made")
        h_ready = sem("h_ready")
        h_turned = sem("h_turned")
        hT_ready = sem("hT_ready")
        y_made = sem("y_made")
        y_ready = sem("y_ready")
        yb_written = [sem(f"yb_written{r}") for r in range(2)]
        comb_ready = sem("comb_ready")
        y_back = [sem(f"y_back{r}") for r in range(RING)]
        first_gated = sem("first_gated")
        out_ready = sem("out_ready")
        out_stored = [sem(f"out_stored{r}") for r in range(2)]

        def gate(eng, s, value):
            eng.wait_ge(s, value)
            eng.sem_inc(gate_passed, 1)

        def dram_block(t, n_blocks, i, r):
            v = t[0:n_blocks * P, :].rearrange("(i r p) d -> i r p d", r=2, p=P)
            return v[bass.ds(i, 1), r].rearrange("a p d -> (a p) d")

        def acc_block(b):
            return acc[:, bass.ds(b, 1), :].rearrange("p a d -> p (a d)")


        def load_spans(eng, regs, n, count):
            eng.load(regs[:2 * count], bounds[0:1, bass.ds(n * 2, 2 * count)])
            return [tuple(eng.snap(g, min_val=0, max_val=NBLK - 1) for g in regs[2 * q:2 * q + 2]) for q in range(count)]

        def if_left(eng, regs):
            eng.wait_ge(left_known, 1)
            eng.reg_mov(regs[0], 0)
            eng.load(regs[1:2], left_i[0:1, 0:1])
            return eng.If_lt(regs[0], regs[1])

        block = ctx.enter_context(nc.Block())

        @block.sync
        def _(sp):
            sp.dma_start(dst_i, dst).then_inc(edges_loaded, 16)
            sp.dma_start(src_t, src).then_inc(src_loaded, 16)
            sp.dma_start(gr_i[0:GP, :], dst_spans).then_inc(spans_loaded, 16)
            sp.wait_ge(pad_zeroed, 1)
            sp.dma_start(acc[:, 0:LASTB, :], x[0:LASTB * P, :].rearrange("(b p) d -> p b d", p=P)).then_inc(x_loaded, 16)
            sp.dma_start(acc[0:TAIL, LASTB, :], x[LASTB * P:N, :]).then_inc(x_loaded, 16)
            for k, w in enumerate((W1, W2)):
                sp.dma_start(gw[:, k], w.rearrange("(k p) n -> p k n", p=P)).then_inc(weights_loaded, 16)
            sp.dma_start(b1col[:], b1).then_inc(weights_loaded, 16)
            sp.dma_start(b2row[:], b2.to_broadcast([P, D])).then_inc(weights_loaded, 16)
            sp.dma_start(rw[:], router.rearrange("(k p) e -> p k e", p=P)).then_inc(weights_loaded, 16)
            sp.wait_ge(bounds_made, 1)
            sp.dma_start(bounds_dram.rearrange("(p q) c -> p (q c)", q=GQ), gbo[0:GP, :]).then_inc(bounds_stored, 16)
            sp.wait_ge(bounds_stored, 16)
            sp.dma_start(bounds, bounds_dram.rearrange("(a g) c -> a (g c)", a=1)).then_inc(bounds_loaded, 16)
            sp.wait_ge(dis_made, 1)
            sp.dma_start(dis_dram.rearrange("b (c n) -> (b c) n", n=LO), dis_hl[0:HI, :]).then_inc(dis_stored, 16)
            sp.wait_ge(dis_stored, 16)
            sp.dma_start(dis_bt[0:NBLK, :], dis_dram).then_inc(dis_back, 16)
            left_regs = [sp.alloc_register(f"sp_left{q}") for q in range(2)]
            with if_left(sp, left_regs):
                for layer in range(2):
                    with sp.Fori(0, NBLK // 2, 1) as i:
                        for r in range(2):
                            sp.wait_ge(parts_made, 2 * i + (NBLK * layer + r + 1))
                            sp.dma_start(dram_block(U[layer], NBLK, i, r).rearrange("p (q d) -> p q d", q=PARTS),
                                         parts[:, :, bass.ds(2 * i + r, 1), :].rearrange("p q a d -> p (q a) d")).then_inc(u_stored[r], 16)
            sp.wait_ge(graph_over, 1)
            sp.dma_start(x_rows[:, 0:LASTB, :], x[0:LASTB * P, :].rearrange("(b p) d -> p b d", p=P)).then_inc(x_again, 16)
            sp.dma_start(x_rows[0:TAIL, LASTB, :], x[LASTB * P:N, :]).then_inc(x_again, 16)
            sp.dma_start(w2s[0:HC], w2.rearrange("(c p) n -> p c n", p=HC)).then_inc(w2_loaded, 16)
            sp.wait_ge(x_used, 1)
            for a, w in enumerate((w1, w3)):
                sp.dma_start(w13[:, a], w.rearrange("(k p) n -> p k n", p=P)).then_inc(w13_loaded, 16)
            sp.wait_ge(sched_ready, 1)
            for r in range(RING):
                sp.wait_ge(scattered[r], 32 * (LASTB // RING + (r == 0)))
            for r in range(2):
                sp.wait_ge(yb_written[r], 16 * NE // 2)
            with sp.Fori(0, NT // 2, 1) as i:
                for r in range(2):
                    row = sp.value_load(sched_i[0:1, 1, bass.ds(2 * i + r, 1)], min_val=0, max_val=NE * REGION - P)
                    sp.wait_ge(tile_turned, 2 * i + (r + 1))
                    sp.dma_start(xg[:, r], lists[bass.ds(row, P), :]).then_inc(tile_loaded[r], 16)
            with sp.Fori(0, LASTB // 2, 1) as i:
                for r in range(2):
                    sp.wait_ge(out_ready, 2 * i + (r + 1))
                    sp.dma_start(dram_block(out, LASTB, i, r), acc_block(2 * i + r)).then_inc(out_stored[r], 16)
            sp.wait_ge(out_ready, LASTB + 1)
            sp.dma_start(out[LASTB * P:N, :], acc[0:TAIL, LASTB, :]).then_inc(out_stored[0], 16)
            sp.wait_ge(out_stored[0], 16 * (LASTB // 2 + 1))
            sp.wait_ge(out_stored[1], 16 * (LASTB // 2))

        @block.gpsimd
        def _(pool):
            nc.gpsimd.iota(iota_i[:], pattern=[[1, P]], base=0, channel_multiplier=0).then_inc(iotas_made, 1)
            nc.gpsimd.iota(part_int[:], pattern=[[0, 1]], base=0, channel_multiplier=1).then_inc(iotas_made, 1)
            left_regs = [pool.alloc_register(f"pool_left{q}") for q in range(2)]
            for layer in range(2):
                pool.wait_ge(cells_used, 2 + NB * BATCHES * (layer + 1))
                with if_left(pool, left_regs):
                    for r in range(2):
                        pool.wait_ge(u_stored[r], 16 * (NBLK // 2) * (layer + 1))
                    with pool.Fori(0, ROUNDS, 1) as k:
                        for r in range(SLOTS):
                            gate(pool, idx_staged[r], k + (layer * ROUNDS + 1))
                            for j in range(JT):
                                pool.indirect_dma_start(out=rows[:, r, j], out_offset=None, in_=U[layer],
                                                        in_offset=bass.IndirectOffsetOnAxis(ap=idx_ring[:, r, j:j + 1], axis=0)).then_inc(rows_landed[r], 16)
            pool.wait_ge(fill_ready, 1)
            for e in range(NE):
                pool.indirect_dma_start(out=lists, out_offset=bass.IndirectOffsetOnAxis(ap=ering_i[:, 0, e:e + 1], axis=0),
                                        in_=yb[:, e % 2], in_offset=None).then_inc(yb_written[e % 2], 16)
            with pool.Fori(0, LASTB // RING, 1) as i:
                for r in range(RING):
                    gate(pool, scatter_ready, RING * i + (r + 1))
                    for k in range(2):
                        pool.indirect_dma_start(out=lists, out_offset=bass.IndirectOffsetOnAxis(ap=ring_i[:, r, k:k + 1], axis=0),
                                                in_=outgoing[r], in_offset=None).then_inc(scattered[r], 16)
            pool.wait_ge(scatter_ready, LASTB + 1)
            for k in range(2):
                pool.indirect_dma_start(out=lists, out_offset=bass.IndirectOffsetOnAxis(ap=ring_i[0:TAIL, 0, k:k + 1], axis=0),
                                        in_=outgoing[0][0:TAIL], in_offset=None).then_inc(scattered[0], 16)
            with pool.Fori(0, NT // 2, 1) as i:
                for r in range(2):
                    gate(pool, y_ready, 2 * i + (r + 2))
                    pool.dma_start(dram_block(y_dram, NT, i, r), yb[:, r]).then_inc(yb_written[r], 16)
            for r in range(2):
                pool.wait_ge(yb_written[r], 16 * (NT // 2 + NE // 2))
            def gather_both(r, n):
                gate(pool, comb_ready, n + 1)
                for k in range(2):
                    pool.indirect_dma_start(out=both[:, r, k], out_offset=None, in_=y_dram,
                                            in_offset=bass.IndirectOffsetOnAxis(ap=ring_i[:, r, k:k + 1], axis=0)).then_inc(y_back[r], 16)

            with pool.Fori(0, LASTB // RING, 1) as i:
                for r in range(RING):
                    gather_both(r, RING * i + r)
            gather_both(0, LASTB)

        @block.scalar
        def _(act):
            act.sem_inc(xT_ready, 1)
            act.sem_inc(cells_ready, 2)
            act.sem_inc(squares_summed, 2)
            left_regs = [act.alloc_register(f"act_left{q}") for q in range(2)]

            def root(n, to, of):
                act.wait_ge(root_asked, n)
                nc.scalar.activation(to, of, ACT.Sqrt).then_inc(root_taken, 1)

            root(1, rstd[:], tmp[:])
            act.wait_ge(weights_loaded, 16 * 5)

            def turned(layer, r, n):
                gate(act, z_turned, n + (NBLK * layer + 3))
                if layer == 1:
                    gate(act, z_times_w, n + (NBLK * layer - 1))
                    for k in range(KC):
                        ins = nc.scalar.activation(zT[:, r, k], psT[r][:, k], ACT.Relu, bias=b1col[:, k:k + 1])
                    ins.then_inc(zT_ready, 1)
                else:
                    nc.scalar.copy(zT[:, r], psT[r]).then_inc(zT_ready, 1)

            def squares(layer, r, n, made, value):
                gate(act, made, value)
                gate(act, squares_summed, n + (NBLK * layer + 1))
                nc.scalar.activation(xg[:, r], acc_block(n), ACT.Square, accum_out=tmp[:, bass.ds(n, 1)]).then_inc(squares_summed, 1)

            def product_of(layer, r, n):
                if layer == 1:
                    squares(1, r, n, product_out, n + (NBLK + 3))
                    return
                gate(act, z_times_w, n + (NBLK * layer + 1))
                if layer == 2:
                    nc.scalar.copy(logits[:, bass.ds(n, 1), :].rearrange("p a e -> p (a e)"), psM[r][:, 0:NE]).then_inc(product_out, 1)
                else:
                    nc.scalar.copy(acc_block(n), psM[r]).then_inc(product_out, 1)

            for layer in range(3):
                if layer == 2:
                    with act.Fori(0, NBLK // 2, 1) as i:
                        for r in range(2):
                            squares(2, r, 2 * i + r, z_made, 2 * i + (r + 1))
                    root(5, rstd[:], tmp[:])
                    root(6, rstd[:], tmp[:])
                turned(layer, 0, 0)
                turned(layer, 1, 1)
                with act.Fori(0, NBLK // 2 - 1, 1) as i:
                    for r in range(2):
                        turned(layer, r, 2 * i + (r + 2))
                        product_of(layer, r, 2 * i + r)
                for r in range(2):
                    product_of(layer, r, NBLK - 2 + r)
                if layer == 0:
                    root(2, dis_hl[0:HI, :], count_row[0:HI, :])
                    act.wait_ge(src_loaded, 16)
                if layer < 2:
                    if layer == 0:
                        with act.Fori(0, NBLK // 2, 1) as i:
                            for r in range(2):
                                squares(0, r, 2 * i + r, product_out, 2 * i + (r + 3))
                    root(3 + layer, top_row[:, 0:1], top_row[:, 0:1])
                    act.wait_ge(scale_made, layer + 1)
                    with act.Fori(0, NBLK // UN, 1) as i:
                        for q in range(UN):
                            b = UN * i + q
                            nc.scalar.activation(parts[:, 0, bass.ds(b, 1), :].rearrange("p a d -> p (a d)"), acc_block(b), ACT.Copy,
                                                 scale=row_scale[:, bass.ds(b, 1)]).then_inc(high_made, 1)
                    def take_cells(n, r):
                        gate(act, cells_counted, n + (NB * BATCHES * layer + 3))
                        gate(act, cells_used, n + (NB * BATCHES * layer + 1))
                        nc.scalar.copy(cells[r][:, 0:8].rearrange("p (a t) n -> p a (t n)", a=2), ps[:, 3 * r:3 * r + 2, :])
                        nc.scalar.copy(cells[r][:, 8:CELLS].rearrange("p t n -> p (t n)"), ps[:, 3 * r + 2, 0:2 * P]).then_inc(cells_ready, 1)

                    with act.Fori(0, NB * BATCHES // 2, 1) as i:
                        for r in range(2):
                            take_cells(2 * i + r, r)
                    take_cells(NB * BATCHES - 1, 0)
                    with if_left(act, left_regs):
                        with act.Fori(0, ROUNDS, 1) as k:
                            for r in range(SLOTS):
                                gate(act, slot_free[r], k + (layer * ROUNDS + 1))
                                nc.scalar.copy(idx_ring[:, r, :], src_t[:, bass.ds((k * SLOTS + r) * JT, JT)]).then_inc(idx_staged[r], 1)
            act.wait_ge(exp_asked, 1)
            nc.scalar.activation(prob, work, ACT.Exp).then_inc(exp_made, 1)

            def silu(n):
                gate(act, gates_made, n + 1)
                gate(act, h_ready, n + 1)
                nc.scalar.activation(s1.rearrange("p (c n) -> p c n", c=2), ps[:, 0:2, 0:HH], ACT.Silu).then_inc(silu_made, 1)

            def turned_out(r, n):
                gate(act, tile_turned, n + 3)
                nc.scalar.copy(xT[:, r], ps[:, 7, 0:KC * P].rearrange("p (k n) -> p k n", k=KC)).then_inc(xT_ready, 1)

            turned_out(0, 0)
            with act.Fori(0, NT // 2 - 1, 1) as i:
                silu(2 * i)
                turned_out(1, 2 * i + 1)
                silu(2 * i + 1)
                turned_out(0, 2 * i + 2)
            silu(NT - 2)
            turned_out(1, NT - 1)
            silu(NT - 1)

        @block.tensor
        def _(pe):
            pe.sem_inc(hots_counted, 2)
            pe.sem_inc(cells_counted, 2)
            pe.sem_inc(cells_used, 2)
            pe.sem_inc(slots_summed, 2)
            pe.sem_inc(first_summed, 2)
            pe.sem_inc(more_summed, 1)
            pe.sem_inc(z_turned, 2)
            pe.sem_inc(tile_turned, 2)
            pe.sem_inc(h_turned, 1)
            pe.sem_inc(y_made, 1)
            pe.wait_ge(consts_made, 1)
            nc.tensor.matmul(psCnt, ones_b[0:1, 0:HI], ones_b[0:1, 0:LO], start=True, stop=True, skip_group_check=True)

            def count(r, n):
                pe.wait_ge(hots_ready, n + 1)
                for t in range(CT):
                    mm = nc.tensor.matmul(psCnt, hot_hi[r][:, :, t], hot_lo[r][:, :, t], start=False, stop=True, skip_group_check=True)
                mm.then_inc(hots_counted, 1)

            pe.wait_ge(weights_loaded, 16 * 5)
            steps = pe.alloc_register("pe_steps")
            pe.reg_mov(steps, 0)
            left_regs = [pe.alloc_register(f"pe_left{q}") for q in range(2)]
            bound_regs = [pe.alloc_register(f"pe_bound{q}") for q in range(2 * STEP + 4)]
            for layer in range(3):
                w = (gw[:, 0], gw[:, 1], rw[:])[layer]

                def turn(r, n):
                    pe.wait_ge(z_scaled, n + (NBLK * layer + 1))
                    for k in range(KC):
                        mm = nc.tensor.transpose(psT[r][:, k], zs[:, r, k * P:(k + 1) * P], ident[:])
                    mm.then_inc(z_turned, 1)

                def times_w(r, n):
                    pe.wait_ge(zT_ready, n + (NBLK * layer + 1))
                    pe.wait_ge(product_out, n + (NBLK * layer + 1))
                    for k in range(KC):
                        mm = nc.tensor.matmul(psM[r][:, 0:NE] if layer == 2 else psM[r], zT[:, r, k], w[:, k],
                                              start=k == 0, stop=k == KC - 1)
                    mm.then_inc(z_times_w, 1)

                turn(0, 0)
                with pe.Fori(0, NBLK // 2 - 1, 1) as i:
                    for r in range(2):
                        turn(1 - r, 2 * i + (r + 1))
                        times_w(r, 2 * i + r)
                        if layer == 0:
                            for q in range(CB):
                                count(q, 2 * CB * i + (CB * r + q))
                turn(1, NBLK - 1)
                for r in range(2):
                    times_w(r, NBLK - 2 + r)
                if layer == 0:
                    for n in range(CB * (NBLK - 2), COUNTS):
                        count(n % 2, n)
                    pe.wait_ge(dis_back, 16)
                    nc.tensor.transpose(psDis, dis_bt[0:NBLK, :], ident[0:NBLK, 0:NBLK]).then_inc(dis_turned, 1)
                if layer == 2:
                    break
                pe.wait_ge(bounds_loaded, 16)
                if layer == 0:
                    pe.wait_ge(product_out, 2 + NBLK)

                    def prefixes(to, oh):
                        nc.tensor.matmul(to[:, 0:GT], upper_b, oh.rearrange("p s t -> p t s"), start=True, stop=True, skip_group_check=True)
                        nc.tensor.matmul(to[:, GT], ones_b[:], oh[:, :, GT - 1], start=False, stop=True, skip_group_check=True)
                        for t in range(GT - 1):
                            nc.tensor.matmul(to[:, t + 1:GT + 1], ones_b[:], oh[:, :, t].unsqueeze(1).to_broadcast([P, GT - t, SC]),
                                             start=False, stop=True, skip_group_check=True)

                    def carry(to, b):
                        return nc.tensor.matmul(to, ones_b[0:1, :], filled[:, bass.ds(b, 1), :].to_broadcast([1, GT + 1, SC]),
                                                start=False, stop=True, skip_group_check=True)

                    def to_slots(to, hot, values):
                        for t in range(GT):
                            mm = nc.tensor.matmul(to, hot[:, :, t], values[:, :, :, t], start=t == 0, stop=t == GT - 1)
                        return mm

                    def first_prefixes(g, p):
                        pe.wait_ge(marks_made, g + 1)
                        prefixes(psPrefix[p], first_bufs[p][1])

                    def first_carry(g, p, b):
                        pe.wait_ge(filled_kept, g + 1)
                        carry(psPrefix[p], b).then_inc(prefix_made, 1)

                    def first_slots(g, p):
                        pe.wait_ge(slot_hots_made, g + 1)
                        pe.wait_ge(slots_added, g + 1)
                        to_slots(psSlot[p], first_bufs[p][5], first_bufs[p][4]).then_inc(slots_summed, 1)

                    def more_slots(q, first, last):
                        with pe.If_lt(bound_regs[2 * q], bound_regs[2 * q + 1]):
                            with pe.Fori(first + 1, last + 1, 1) as b:
                                n = pe.snap(steps)
                                pe.wait_ge(more_marks_made, n + 1)
                                prefixes(psMorePrefix, more_bufs[1])
                                carry(psMorePrefix, b).then_inc(more_prefix_made, 1)
                                pe.wait_ge(more_slot_hots_made, n + 1)
                                to_slots(psMoreSlot, more_bufs[5], more_bufs[4]).then_inc(more_slots_summed, 1)
                                pe.wait_ge(more_filled_kept, n + 1)
                                pe.reg_add(steps, steps, 1)

                    def span_step(g, p, q, spans, last=False):
                        if not last:
                            first_prefixes(g + 1, 1 - p)
                        more_slots(q, *spans[q])
                        if not last:
                            first_carry(g + 1, 1 - p, spans[q + 1][0])
                        first_slots(g, p)

                    spans = load_spans(pe, bound_regs, 0, 2)
                    first_prefixes(0, 0)
                    first_carry(0, 0, spans[0][0])
                    span_step(0, 0, 0, spans)
                    with pe.Fori(0, TURNS, 1) as k:
                        spans = load_spans(pe, bound_regs, k * STEP + 1, STEP + 1)
                        for q in range(STEP):
                            span_step(k * STEP + (q + 1), (q + 1) % 2, q, spans)
                    spans = load_spans(pe, bound_regs, SPANS - 1, 1)
                    span_step(SPANS - 1, (SPANS - 1) % 2, 0, spans, last=True)
                    pe.reg_mov(steps, 0)
                    pe.wait_ge(left_asked, 1)
                    nc.tensor.matmul(psLeft, ones[:], left_col[:], start=True, stop=True).then_inc(left_summed, 1)

                def build(r, n):
                    pe.wait_ge(cell_hots_made, n + (NB * BATCHES * layer + 1))
                    pe.wait_ge(cells_ready, n + (NB * BATCHES * layer + 1))
                    for c in range(CELLS):
                        mm = nc.tensor.matmul(ps_cell(r, c), cell_hot[r][0][:, :, c], cell_hot[r][1][:, :, c], start=True, stop=True, skip_group_check=True)
                    mm.then_inc(cells_counted, 1)

                def aggregate(q, n, d, dr):
                    pe.wait_ge(cells_ready, n + (NB * BATCHES * layer + 3))
                    if q == 0:
                        pe.wait_ge(sums_taken, d + (NB * layer + 1))
                    used = min(CELLS, NB - q * CELLS)
                    for c in range(used):
                        for part in range(PARTS):
                            mm = nc.tensor.matmul(psSum[dr], cells[(BATCHES * dr + q) % 2][:, c], parts[:, part, q * CELLS + c],
                                                  start=q == 0 and c == 0 and part == 0,
                                                  stop=q == BATCHES - 1 and c == used - 1 and part == PARTS - 1, skip_group_check=True)
                    mm.then_inc(cells_used, 1)

                def rounds(d, dr, last=False):
                    for q in range(BATCHES):
                        n = BATCHES * d + q
                        if not (last and q == BATCHES - 1):
                            build((BATCHES * dr + q + 1) % 2, n + 1)
                        aggregate(q, n, d, dr)

                pe.wait_ge(tops_made, layer + 1)
                nc.tensor.transpose(psTop, left_col[:], ident[:]).then_inc(tops_turned, 1)
                pe.wait_ge(top_made, layer + 1)
                nc.tensor.matmul(psScale, ones[0:1, :], top_row[:, 0:1], start=True, stop=True).then_inc(top_spread, 1)
                build(0, 0)
                pe.wait_ge(parts_made, NBLK * (layer + 1))
                with pe.Fori(0, NB // 2, 1) as i:
                    for dr in range(2):
                        rounds(2 * i + dr, dr)
                rounds(NB - 1, 0, last=True)

                def sum_first(k, r):
                    n = k * SLOTS + (layer * GROUPS + r)
                    pe.wait_ge(rows_landed[r % SLOTS], k * (16 * JT) + 16 * JT * (layer * ROUNDS + 1 + r // SLOTS))
                    pe.wait_ge(first_hot_ready, n + 1)
                    pe.wait_ge(first_added, n + 1)
                    for j in range(JT):
                        for q in range(PARTS):
                            mm = nc.tensor.matmul(psFirst[r % 2], first_hot[r % 2][:, j], rows[:, r % SLOTS, j, q * D:(q + 1) * D],
                                                  start=j + q == 0, stop=j == JT - 1 and q == PARTS - 1)
                    mm.then_inc(first_summed, 1)

                def sum_more(r, first, last):
                    with pe.If_lt(bound_regs[2 * (r // PAIR)], bound_regs[2 * (r // PAIR) + 1]):
                        with pe.Fori(first + 1, last + 1, 1):
                            n = pe.snap(steps)
                            pe.wait_ge(more_hot_ready, n + 1)
                            pe.wait_ge(more_added, n + 1)
                            for j in range(JT):
                                for q in range(PARTS):
                                    mm = nc.tensor.matmul(psMore, more_hot[:, j], rows[:, r, j, q * D:(q + 1) * D],
                                                          start=j + q == 0, stop=j == JT - 1 and q == PARTS - 1)
                            mm.then_inc(more_summed, 1)
                            pe.reg_add(steps, steps, 1)

                pe.wait_ge(sums_taken, 2 + NB * (layer + 1))
                with if_left(pe, left_regs):
                    sum_first(0, 0)
                    with pe.Fori(0, ROUNDS - 1, 1) as k:
                        spans = load_spans(pe, bound_regs, k * (SLOTS // PAIR), SLOTS // PAIR)
                        for r in range(SLOTS):
                            sum_first(k, r + 1)
                            sum_more(r, *spans[r // PAIR])
                    spans = load_spans(pe, bound_regs, (ROUNDS - 1) * (SLOTS // PAIR), SLOTS // PAIR)
                    for r in range(SLOTS):
                        if r + 1 < SLOTS:
                            sum_first(ROUNDS - 1, r + 1)
                        sum_more(r, *spans[r // PAIR])
            pe.wait_ge(mask_ready, 1)
            flat = work.rearrange("p b e -> p (b e)")
            nc.tensor.matmul(ps[:, 4, 0:NBLK * NE], upper[:], flat, start=True, stop=True)
            nc.tensor.matmul(ps[:, 5, 0:NBLK * NE], ones[:], flat, start=True, stop=True).then_inc(ranks_made, 1)

            def turn_tile(r, i, n):
                pe.wait_ge(tile_loaded[r], i * 16 + 16)
                pe.wait_ge(xT_ready, n + 1)
                for k in range(KC):
                    mm = nc.tensor.transpose(ps[:, 7, k * P:(k + 1) * P], xg[:, r, k * P:(k + 1) * P], ident[:])
                mm.then_inc(tile_turned, 1)

            def hidden(r, n, e):
                pe.wait_ge(xT_ready, n + 2)
                pe.wait_ge(h_ready, n + 1)
                for a in range(2):
                    for c in range(2):
                        for k in range(KC):
                            mm = nc.tensor.matmul(ps[:, 2 * a + c, 0:HH], xT[:, r, k],
                                                  w13[:, a, k, bass.ds(e * HP + c * HH, HH)], start=k == 0, stop=k == KC - 1)
                    mm.then_inc((gates_made, hidden_made)[a], 1)

            def turn_h(n):
                pe.wait_ge(h_ready, n + 2)
                pe.wait_ge(hT_ready, n + 1)
                for c in range(NHC):
                    mm = nc.tensor.transpose(ps[0:HC, 4 + c // 3, (c % 3) * P:(c % 3 + 1) * P], h[:, c * HC:(c + 1) * HC], ident[:])
                mm.then_inc(h_turned, 1)

            def out_rows(n, e):
                pe.wait_ge(hT_ready, n + 2)
                pe.wait_ge(y_ready, n + 1)
                for c in range(NHC):
                    mm = nc.tensor.matmul(ps[:, 6, 0:D], hT[0:HC, c, :], w2s[0:HC, c, bass.ds(e * D, D)], start=c == 0, stop=c == NHC - 1)
                mm.then_inc(y_made, 1)

            pe.wait_ge(sched_ready, 1)
            pe.wait_ge(w13_loaded, 32)
            pe.wait_ge(w2_loaded, 16)
            e_regs = [pe.alloc_register(f"pe_expert{q}") for q in range(4)]

            def load_experts(regs, n):
                pe.load(regs, sched_i[0:1, 0, bass.ds(n, 2)])

            def expert(q):
                return pe.snap(e_regs[q], min_val=0, max_val=NE - 1)

            load_experts(e_regs[0:2], 0)
            turn_tile(0, 0, 0)
            hidden(0, 0, expert(0))
            turn_tile(1, 0, 1)
            hidden(1, 1, expert(1))
            turn_h(0)
            turn_tile(0, 1, 2)
            with pe.Fori(0, NT // 2 - 2, 1) as i:
                load_experts(e_regs[2:4], 2 * i + 2)
                hidden(0, 2 * i + 2, expert(2))
                turn_h(2 * i + 1)
                turn_tile(1, i + 1, 2 * i + 3)
                out_rows(2 * i, expert(0))
                hidden(1, 2 * i + 3, expert(3))
                turn_h(2 * i + 2)
                turn_tile(0, i + 2, 2 * i + 4)
                out_rows(2 * i + 1, expert(1))
                for q in range(2):
                    pe.reg_mov(e_regs[q], e_regs[2 + q])
            load_experts(e_regs[2:4], NT - 2)
            hidden(0, NT - 2, expert(2))
            turn_h(NT - 3)
            turn_tile(1, NT // 2 - 1, NT - 1)
            out_rows(NT - 4, expert(0))
            hidden(1, NT - 1, expert(3))
            turn_h(NT - 2)
            out_rows(NT - 3, expert(1))
            turn_h(NT - 1)
            out_rows(NT - 2, expert(2))
            out_rows(NT - 1, expert(3))

        @block.vector
        def _(dve):
            v = nc.vector
            dve.sem_inc(first_added, 2)
            dve.sem_inc(slots_added, 2)
            dve.sem_inc(sums_taken, 2)
            dve.sem_inc(more_added, 1)
            dve.sem_inc(product_out, 2)
            dve.sem_inc(h_ready, 1)
            dve.sem_inc(hT_ready, 1)
            dve.sem_inc(y_ready, 1)
            for r in range(SLOTS):
                dve.sem_inc(slot_free[r], 1)

            done = [0]

            def then(ins):
                ins.then_inc(dve_step, 1)
                done[0] += 1
                dve.wait_ge(dve_step, done[0])

            v.memset(acc[:, LASTB:NBLK, :], 0.0).then_inc(pad_zeroed, 1)
            v.memset(ones[:], 1.0)
            then(v.memset(ones_b[:], 1.0))
            dve.wait_ge(iotas_made, 2)
            v.tensor_copy(iota[:], iota_i[:])
            then(v.tensor_copy(part[:], part_int[:]))
            v.tensor_scalar(ident[:], iota[:], part[:, 0:1], None, ALU.is_equal)
            then(v.tensor_scalar(upper[:], iota[:], part[:, 0:1], None, ALU.is_gt))
            v.tensor_copy(numbers, iota[:, 0:HI].unsqueeze(2).to_broadcast([P, HI, CT]))
            v.tensor_copy(upper_b, upper[:])
            v.tensor_scalar(numbers1, iota[:].unsqueeze(2).to_broadcast([P, P, CELLS]), 1.0, None, ALU.add)
            v.memset(slots, 0.0)
            v.memset(loops, 1.0)
            v.memset(filled, 0.0).then_inc(filled_kept, 1)
            v.tensor_scalar(base_code[:], iota[:, 0:NBLK], float(CODE), None, ALU.mult)
            then(v.tensor_scalar(base[:], iota[:, 0:NBLK], float(P), None, ALU.mult))
            v.tensor_scalar(valid[:], base[:], part[:, 0:1], float(N), ALU.add, ALU.is_lt).then_inc(consts_made, 1)
            dve.wait_ge(edges_loaded, 16)
            v.tensor_copy(dst_f, dst_i)
            v.tensor_scalar(lo_i, dst_i, LO - 1, None, ALU.bitwise_and)
            then(v.tensor_scalar(hi_i, dst_i, 6, None, ALU.logical_shift_right))
            v.tensor_copy(lo_b, lo_i)
            then(v.tensor_copy(hi_b, hi_i))
            dve.wait_ge(src_loaded, 16)
            number_i = hi_i
            differ = lo_i.bitcast(F32)
            then(v.tensor_tensor(differ, src_t, dst_i, ALU.not_equal))
            then(v.tensor_scalar(number_i, src_t, P - 1, None, ALU.bitwise_and))
            then(v.tensor_tensor(code, number_i, differ, ALU.mult))
            then(v.tensor_scalar(src1, code, 1.0, None, ALU.add))
            then(v.tensor_scalar(number_i, dst_i, P - 1, None, ALU.bitwise_and))
            then(v.tensor_scalar(dst1, number_i, 1.0, None, ALU.add))
            then(v.tensor_tensor(code, number_i, differ, ALU.mult))
            then(v.tensor_tensor(rank1, dst1, code, ALU.subtract))
            then(v.tensor_scalar(number_i, src_t, 7, None, ALU.logical_shift_right))
            then(v.tensor_scalar(code, number_i, float(-NBLK), None, ALU.add))
            then(v.tensor_tensor(differ, code, differ, ALU.mult))
            then(v.tensor_scalar(number_i, dst_i, 7, None, ALU.logical_shift_right))
            then(v.scalar_tensor_tensor(code, number_i, float(CODE), differ, ALU.mult, ALU.add))
            then(v.tensor_scalar(code, code, float(NBLK + 1), None, ALU.add))
            dve.wait_ge(spans_loaded, 16)
            gr = gr_i[0:GP, :].rearrange("p (q e) -> p q e", q=GQ)
            v.tensor_reduce(gbi[0:GP, 0:GQ], gr, AX, ALU.min)
            then(v.tensor_reduce(gbi[0:GP, GQ:2 * GQ], gr, AX, ALU.max))
            then(v.tensor_scalar(gbi[0:GP, :], gbi[0:GP, :], 7, None, ALU.logical_shift_right))
            pair = gbo[0:GP, :].rearrange("p (q c) -> p q c", c=2)
            v.tensor_copy(pair[:, :, 0], gbi[0:GP, 0:GQ])
            v.tensor_copy(pair[:, :, 1], gbi[0:GP, GQ:2 * GQ]).then_inc(bounds_made, 1)

            def moments():
                v.tensor_tensor(mean[:], bn[:, :, 1], bn[:, :, 4], ALU.add)
                v.tensor_tensor(var[:], bn[:, :, 2], bn[:, :, 5], ALU.add)
                then(v.tensor_tensor(tmp[:], bn[:, :, 1], bn[:, :, 4], ALU.subtract))
                v.tensor_scalar(mean[:], mean[:], 0.5, None, ALU.mult)
                then(v.tensor_tensor(tmp[:], tmp[:], tmp[:], ALU.mult))
                then(v.scalar_tensor_tensor(var[:], tmp[:], float(D // 4), var[:], ALU.mult, ALU.add))
                then(v.tensor_scalar(var[:], var[:], 1.0 / D, None, ALU.mult))

            def one_over_std(n):
                v.tensor_scalar(tmp[:], var[:], EPS_LN, None, ALU.add).then_inc(root_asked, 1)
                dve.wait_ge(root_taken, n)
                then(v.reciprocal(rstd[:], rstd[:]))

            dve.wait_ge(x_loaded, 32)
            def stats_of(b):
                return v.bn_stats(bn[:, bass.ds(b, 1), :].rearrange("p a q -> p (a q)"), acc_block(b))

            with dve.Fori(0, NBLK // UN, 1) as i:
                for q in range(UN):
                    stats_of(UN * i + q).then_inc(dve_step, 1)
            done[0] += NBLK
            dve.wait_ge(dve_step, done[0])
            moments()
            one_over_std(1)
            dve.wait_ge(weights_loaded, 16 * 5)
            steps = dve.alloc_register("dve_steps")
            dve.reg_mov(steps, 0)
            more_steps = dve.alloc_register("dve_more_steps")
            dve.reg_mov(more_steps, 0)
            left_regs = [dve.alloc_register(f"dve_left{q}") for q in range(2)]
            bound_regs = [dve.alloc_register(f"dve_bound{q}") for q in range(2 * STEP + 4)]
            for layer in range(3):
                if layer == 2:
                    def z_block(b):
                        return v.scalar_tensor_tensor(acc_block(b), acc_block(b), dis_unscaled[:, bass.ds(b, 1)], b2row[:], ALU.mult, ALU.add)

                    with dve.Fori(0, NBLK // UN, 1) as i:
                        for q in range(UN):
                            z_block(UN * i + q).then_inc(z_made, 1)
                    dve.wait_ge(squares_summed, 2 + 3 * NBLK)
                    v.memset(tick[:, 0:1], 0.0).then_inc(root_asked, 1)
                    dve.wait_ge(root_taken, 5)
                    then(v.tensor_scalar(rstd[:], rstd[:], 1e-12, None, ALU.max))
                    then(v.reciprocal(red[:], rstd[:]))

                    def residual(rows, b, x_part):
                        return v.scalar_tensor_tensor(rows, rows, red[0:rows.shape[0], bass.ds(b, 1)], x_part, ALU.mult, ALU.add)

                    dve.wait_ge(x_again, 32)
                    with dve.Fori(0, LASTB // XU, 1) as i:
                        for r in range(XU):
                            b = XU * i + r
                            residual(acc_block(b), b, x_rows[:, bass.ds(b, 1), :].rearrange("p a d -> p (a d)")).then_inc(dve_step, 1)
                        for r in range(XU):
                            gate(dve, dve_step, XU * i + (done[0] + r + 1))
                            stats_of(XU * i + r)
                    done[0] += LASTB
                    v.memset(tick[:, 0:1], 0.0)
                    then(residual(acc[0:TAIL, LASTB, :], LASTB, x_rows[0:TAIL, LASTB, :]))
                    stats_of(LASTB).then_inc(x_used, 1)
                    dve.wait_ge(x_used, 1)
                    moments()
                    one_over_std(6)

                def scale(r, n):
                    gate(dve, z_turned, n + (NBLK * layer + 1))
                    if layer == 1:
                        v.tensor_scalar(zs[:, r], acc_block(n), dis_unscaled[:, bass.ds(n, 1)], None, ALU.mult).then_inc(z_scaled, 1)
                    else:
                        v.tensor_scalar(zs[:, r], acc_block(n), mean[:, bass.ds(n, 1)], rstd[:, bass.ds(n, 1)], ALU.subtract, ALU.mult).then_inc(z_scaled, 1)

                def count(r, n):
                    gate(dve, hots_counted, n + 1)
                    v.tensor_tensor(hot_hi[r], hi_b[:, bass.ds(n * CT, CT)].unsqueeze(1).to_broadcast([P, HI, CT]), numbers, ALU.is_equal)
                    v.tensor_tensor(hot_lo[r], lo_b[:, bass.ds(n * CT, CT)].unsqueeze(1).to_broadcast([P, LO, CT]), numbers[:, 0:LO], ALU.is_equal).then_inc(hots_ready, 1)

                def times_dis(r, n):
                    gate(dve, z_times_w, n + (NBLK * layer + 1))
                    v.tensor_scalar(acc_block(n), psM[r], dis[:, bass.ds(n, 1)], None, ALU.mult).then_inc(product_out, 1)

                for r in range(2):
                    scale(r, r)
                with dve.Fori(0, NBLK // 2 - 1, 1) as i:
                    for r in range(2):
                        if layer == 0:
                            for q in range(CB):
                                count(q, 2 * CB * i + (CB * r + q))
                        scale(r, 2 * i + (r + 2))
                        if layer == 1:
                            times_dis(r, 2 * i + r)
                if layer == 1:
                    for r in range(2):
                        times_dis(r, NBLK - 2 + r)
                if layer == 0:
                    for n in range(CB * (NBLK - 2), COUNTS):
                        count(n % 2, n)
                    dve.wait_ge(hots_counted, 2 + COUNTS)
                    v.tensor_copy(count_row[0:HI, :], psCnt).then_inc(root_asked, 1)
                    dve.wait_ge(root_taken, 2)
                    v.reciprocal(dis_hl[0:HI, :], dis_hl[0:HI, :]).then_inc(dis_made, 1)
                    dve.wait_ge(bounds_loaded, 16)

                    def tiles_of(g):
                        return bass.ds(g * GT, GT)

                    def codes_less(bufs, g, b):
                        return v.tensor_scalar(bufs[0], code[:, tiles_of(g)], base_code[:, bass.ds(b, 1)], None, ALU.subtract)

                    def marks(bufs):
                        return v.tensor_tensor(bufs[1], bufs[0].unsqueeze(1).to_broadcast([P, SC, GT]), numbers1[:, 0:SC, 0:GT], ALU.is_equal)

                    def before(bufs, prefix):
                        return v.tensor_tensor(bufs[2], prefix[:, 0:GT, 0:NBLK], bufs[1][:, 0:NBLK, :].rearrange("p s t -> p t s"), ALU.mult)

                    def before_sum(bufs):
                        return v.tensor_reduce(bufs[3], bufs[2], AX, ALU.add)

                    def rank(bufs, g):
                        at = rank1[:, tiles_of(g)]
                        return v.scalar_tensor_tensor(at, bufs[3], float(P), at, ALU.min, ALU.add)

                    def values(bufs, q, g):
                        return v.tensor_tensor(bufs[4][:, q], bufs[1], (src1, dst1)[q][:, tiles_of(g)].unsqueeze(1).to_broadcast([P, SC, GT]), ALU.mult)

                    def slot_hots(bufs, g):
                        return v.tensor_tensor(bufs[5], rank1[:, tiles_of(g)].unsqueeze(1).to_broadcast([P, P, GT]), numbers1[:, :, 0:GT], ALU.is_equal)

                    def keep_filled(prefix, b):
                        return v.tensor_copy(filled[:, bass.ds(b, 1), :].rearrange("p a s -> p (a s)"), prefix[0:1, GT])

                    def add_slots(sums, b):
                        at = slots[:, bass.ds(b, 1)].rearrange("p a q s -> p (a q) s")
                        v.tensor_tensor(at, at, sums[:, :, 0:NBLK], ALU.add)
                        return v.tensor_tensor(loops[:, bass.ds(b, 1)], loops[:, bass.ds(b, 1)], sums[:, 0, NBLK:SC], ALU.add)

                    def first_codes(g, p, b):
                        codes_less(first_bufs[p], g, b).then_inc(bucket_step, 1)

                    def first_add(g, p, b):
                        gate(dve, slots_summed, g + 3)
                        add_slots(psSlot[p], b).then_inc(slots_added, 1)

                    def more_ranks(g, q, first, last):
                        with dve.If_lt(bound_regs[2 * q], bound_regs[2 * q + 1]):
                            with dve.Fori(first + 1, last + 1, 1) as b:
                                m = dve.snap(steps)
                                at = dve.snap(more_steps)

                                def stepped(ins, n):
                                    ins.then_inc(more_step, 1)
                                    gate(dve, more_step, at + n)

                                stepped(codes_less(more_bufs, g, b), 1)
                                marks(more_bufs).then_inc(more_marks_made, 1)
                                gate(dve, more_marks_made, m + 1)
                                for a in range(2):
                                    values(more_bufs, a, g)
                                gate(dve, more_prefix_made, m + 1)
                                before(more_bufs, psMorePrefix).then_inc(more_step, 1)
                                keep_filled(psMorePrefix, b).then_inc(more_filled_kept, 1)
                                gate(dve, more_step, at + 2)
                                stepped(before_sum(more_bufs), 3)
                                stepped(rank(more_bufs, g), 4)
                                slot_hots(more_bufs, g).then_inc(more_slot_hots_made, 1)
                                gate(dve, more_slots_summed, m + 1)
                                stepped(add_slots(psMoreSlot, b), 5)
                                dve.reg_add(steps, steps, 1)
                                dve.reg_add(more_steps, more_steps, 5)

                    def span_step(g, p, q, spans, first=False, last=False):
                        bufs = first_bufs[p]
                        n = g * 4 + (0 if last else 1)
                        if not last:
                            first_codes(g + 1, 1 - p, spans[q + 1][0])
                        values(bufs, 0, g)
                        if not last:
                            gate(dve, bucket_step, n + 1)
                            marks(first_bufs[1 - p]).then_inc(marks_made, 1)
                        gate(dve, prefix_made, g + 1)
                        before(bufs, psPrefix[p]).then_inc(bucket_step, 1)
                        keep_filled(psPrefix[p], spans[q][0]).then_inc(filled_kept, 1)
                        more_ranks(g, q, *spans[q])
                        gate(dve, bucket_step, n + 2)
                        before_sum(bufs).then_inc(bucket_step, 1)
                        if not first:
                            first_add(g - 1, 1 - p, spans[q - 1][0])
                        gate(dve, bucket_step, n + 3)
                        rank(bufs, g).then_inc(bucket_step, 1)
                        values(bufs, 1, g)
                        gate(dve, bucket_step, n + 4)
                        slot_hots(bufs, g).then_inc(slot_hots_made, 1)

                    spans = load_spans(dve, bound_regs, 0, 2)
                    first_codes(0, 0, spans[0][0])
                    dve.wait_ge(bucket_step, 1)
                    marks(first_bufs[0]).then_inc(marks_made, 1)
                    dve.wait_ge(marks_made, 1)
                    span_step(0, 0, 0, spans, first=True)
                    with dve.Fori(0, TURNS, 1) as k:
                        spans = load_spans(dve, bound_regs, k * STEP, STEP + 2)
                        for q in range(1, STEP + 1):
                            span_step(k * STEP + q, q % 2, q, spans)
                    spans = load_spans(dve, bound_regs, SPANS - 2, 2)
                    span_step(SPANS - 1, (SPANS - 1) % 2, 1, spans, last=True)
                    first_add(SPANS - 1, (SPANS - 1) % 2, spans[1][0])
                    dve.wait_ge(slots_added, 2 + SPANS)
                    dve.reg_mov(steps, 0)
                    left = lo_i.bitcast(F32)
                    then(v.tensor_scalar(left, rank1, float(P + 1), None, ALU.is_ge))
                    v.tensor_reduce(left_col[:], left, AX, ALU.add).then_inc(left_asked, 1)
                    then(v.tensor_scalar(dst_f, dst_f, 1.0, None, ALU.add))
                    then(v.tensor_tensor(dst_f, dst_f, left, ALU.mult))
                    then(v.tensor_scalar(dst_f, dst_f, -1.0, None, ALU.add))
                    dve.wait_ge(left_summed, 1)
                    v.tensor_copy(left_i[:], psLeft).then_inc(left_known, 1)
                    dve.wait_ge(dis_turned, 1)
                    then(v.tensor_copy(dis[:], psDis))
                    dve.wait_ge(product_out, 2 + NBLK)
                if layer == 2:
                    break

                dve.wait_ge(squares_summed, 2 + NBLK * (layer + 1))
                if layer == 0:
                    for _ in range(2):
                        then(v.tensor_tensor(tmp[:], tmp[:], dis[:], ALU.mult))
                v.tensor_reduce(left_col[:], tmp[:], AX, ALU.max).then_inc(tops_made, 1)
                dve.wait_ge(tops_turned, layer + 1)
                then(v.tensor_copy(top_row, psTop))
                v.tensor_reduce(top_row[:, 0:1], top_row, AX, ALU.max).then_inc(root_asked, 1)
                dve.wait_ge(root_taken, 3 + layer)
                v.tensor_scalar(top_row[:, 0:1], top_row[:, 0:1], 1e-18, 2.0 ** -14, ALU.max, ALU.mult).then_inc(top_made, 1)
                dve.wait_ge(top_spread, layer + 1)
                v.tensor_scalar(dis_unscaled[:], dis[:], psScale, None, ALU.mult)
                then(v.reciprocal(left_col[:], psScale))
                then(v.tensor_scalar(row_scale, dis[:] if layer == 0 else ones[:, 0:NBLK], left_col[:], None, ALU.mult))
                v.tensor_tensor(scaled_loops, loops, row_scale, ALU.mult).then_inc(scale_made, 1)
                with dve.Fori(0, NBLK // UN, 1) as i:
                    for q in range(UN):
                        b = UN * i + q
                        gate(dve, high_made, b + (NBLK * layer + 1))
                        v.scalar_tensor_tensor(parts[:, 1, bass.ds(b, 1), :].rearrange("p a d -> p (a d)"), acc_block(b), row_scale[:, bass.ds(b, 1)],
                                               parts[:, 0, bass.ds(b, 1), :].rearrange("p a d -> p (a d)"), ALU.mult, ALU.subtract).then_inc(parts_made, 1)

                def cell_hots(q, r, n, d):
                    gate(dve, cells_counted, n + (NB * BATCHES * layer + 1))
                    for a in range(2):
                        ins = v.tensor_tensor(cell_hot[r][a],
                                              slots[:, bass.ds(d, 1), a, q * CELLS:(q + 1) * CELLS].to_broadcast([P, P, CELLS]),
                                              numbers1, ALU.is_equal)
                    ins.then_inc(cell_hots_made, 1)

                def take_sums(d, dr):
                    gate(dve, cells_used, BATCHES * d + (NB * BATCHES * layer + BATCHES + 2))
                    v.scalar_tensor_tensor(acc_block(d), acc_block(d), scaled_loops[:, bass.ds(d, 1)], psSum[dr], ALU.mult, ALU.add).then_inc(sums_taken, 1)

                def block_hots(d, dr, n0, before):
                    for q in range(BATCHES):
                        cell_hots(q, (BATCHES * dr + q) % 2, n0 + q, d)
                        if q == 2 and before is not None:
                            take_sums(before, 1 - dr)

                block_hots(0, 0, 0, None)
                with dve.Fori(0, NB // 2, 1) as i:
                    block_hots(2 * i + 1, 1, 2 * BATCHES * i + BATCHES, 2 * i)
                    block_hots(2 * i + 2, 0, 2 * BATCHES * i + 2 * BATCHES, 2 * i + 1)
                take_sums(NB - 1, 0)
                dve.wait_ge(sums_taken, 2 + NB * (layer + 1))

                def hots(to, k, r, b):
                    for j in range(JT):
                        ins = v.tensor_scalar(to[:, j], iota[:], base[:, bass.ds(b, 1)],
                                              dst_f[:, bass.ds(k * (SLOTS * JT) + (r * JT + j), 1)], ALU.add, ALU.is_equal)
                    return ins

                def first_hots(k, r, b):
                    gate(dve, first_summed, k * SLOTS + (layer * GROUPS + r + 1))
                    hots(first_hot[r % 2], k, r, b).then_inc(first_hot_ready, 1)

                def add_sums(k, r, first, last):
                    n = k * SLOTS + (layer * GROUPS + r)
                    gate(dve, first_summed, n + 3)
                    gate(dve, first_added, n + 2)
                    v.tensor_tensor(acc_block(first), acc_block(first), psFirst[r % 2], ALU.add).then_inc(first_added, 1)
                    with dve.If_lt(bound_regs[2 * (r // PAIR)], bound_regs[2 * (r // PAIR) + 1]):
                        with dve.Fori(first + 1, last + 1, 1) as b:
                            m = dve.snap(steps)
                            hots(more_hot, k, r, b).then_inc(more_hot_ready, 1)
                            gate(dve, more_summed, m + 2)
                            v.tensor_tensor(acc_block(b), acc_block(b), psMore, ALU.add).then_inc(more_added, 1)
                            gate(dve, more_added, m + 2)
                            dve.reg_add(steps, steps, 1)
                    v.memset(tick[:, r:r + 1], 0.0).then_inc(slot_free[r], 1)

                with if_left(dve, left_regs):
                    spans = load_spans(dve, bound_regs, 0, 1)
                    first_hots(0, 0, spans[0][0])
                    with dve.Fori(0, ROUNDS - 1, 1) as k:
                        spans = load_spans(dve, bound_regs, k * (SLOTS // PAIR), SLOTS // PAIR + 1)
                        for r in range(SLOTS):
                            first_hots(k, r + 1, spans[(r + 1) // PAIR][0])
                            add_sums(k, r, *spans[r // PAIR])
                    spans = load_spans(dve, bound_regs, (ROUNDS - 1) * (SLOTS // PAIR), SLOTS // PAIR)
                    for r in range(SLOTS):
                        if r + 1 < SLOTS:
                            first_hots(ROUNDS - 1, r + 1, spans[(r + 1) // PAIR][0])
                        add_sums(ROUNDS - 1, r, *spans[r // PAIR])
                    dve.wait_ge(first_added, 2 + GROUPS * (layer + 1))
                if layer == 1:
                    v.memset(tick[:, 0:1], 0.0).then_inc(graph_over, 1)

            dve.wait_ge(product_out, 2 + 3 * NBLK)

            def by_token(t):
                return t.unsqueeze(2).to_broadcast([P, NBLK, NE])

            def by_expert(t):
                return t.unsqueeze(1).to_broadcast([P, NBLK, NE])

            e_iota = by_expert(iota[:, 0:NE])
            then(v.tensor_reduce(red[:], logits, AX, ALU.max))
            v.tensor_tensor(work, logits, by_token(red[:]), ALU.subtract).then_inc(exp_asked, 1)
            dve.wait_ge(exp_made, 1)
            then(v.tensor_reduce(red[:], prob, AX, ALU.add))
            then(v.reciprocal(red[:], red[:]))
            then(v.tensor_tensor(prob, prob, by_token(red[:]), ALU.mult))
            for k in range(2):
                then(v.tensor_reduce(gate_p[k][:], prob, AX, ALU.max))
                then(v.tensor_tensor(work, prob, by_token(gate_p[k][:]), ALU.is_equal))
                then(v.scalar_tensor_tensor(work, work, float(-NE), e_iota, ALU.mult, ALU.add))
                then(v.tensor_reduce(red[:], work, AX, ALU.min))
                then(v.tensor_tensor(mask[k][:], work, by_token(red[:]), ALU.is_equal))
                if k == 0:
                    then(v.scalar_tensor_tensor(prob, mask[0][:], -2.0, prob, ALU.mult, ALU.add))
            then(v.tensor_tensor(red[:], gate_p[0][:], gate_p[1][:], ALU.add))
            then(v.tensor_scalar(red[:], red[:], 1e-9, None, ALU.add))
            then(v.reciprocal(red[:], red[:]))
            for k in range(2):
                v.tensor_tensor(gate_p[k][:], gate_p[k][:], red[:], ALU.mult)
                then(v.tensor_tensor(mask[k][:], mask[k][:], by_token(valid[:]), ALU.mult))
            v.tensor_tensor(work, mask[0][:], mask[1][:], ALU.add).then_inc(mask_ready, 1)
            v.memset(yb[:], 0.0)
            dve.wait_ge(ranks_made, 1)
            then(v.tensor_copy(totals[0][:], psTotal))
            cur, reach = 0, 1
            while reach < NBLK:
                v.tensor_copy(totals[1 - cur][:, 0:reach], totals[cur][:, 0:reach])
                then(v.tensor_tensor(totals[1 - cur][:, reach:], totals[cur][:, reach:], totals[cur][:, :NBLK - reach], ALU.add))
                cur, reach = 1 - cur, 2 * reach
            scan = totals[cur]
            count = scan[:, NBLK - 1, :]
            first_row = ering[:, 0, :]
            then(v.tensor_scalar(first_row, iota[:, 0:NE], float(REGION), None, ALU.mult))
            then(v.tensor_tensor(ering[:, 1, :], count, first_row, ALU.add))
            v.tensor_scalar(ering_i[:, 0, :], ering[:, 1, :], part[:, 0:1], None, ALU.add).then_inc(fill_ready, 1)
            then(v.tensor_tensor(work, psWithin, scan, ALU.add))
            then(v.tensor_tensor(work, work, psTotal, ALU.subtract))
            then(v.tensor_tensor(work, work, by_expert(first_row), ALU.add))
            for k in range(2):
                then(v.tensor_tensor(prob, mask[k][:], work, ALU.mult))
                then(v.tensor_reduce(pos[:, :, k], prob, AX, ALU.add))
            then(v.tensor_copy(pos_i[:], pos[:]))

            def for_scatter(b, r):
                v.tensor_scalar(outgoing[r], acc_block(b), mean[:, bass.ds(b, 1)], rstd[:, bass.ds(b, 1)], ALU.subtract, ALU.mult)
                v.tensor_copy(ring_i[:, r, :], pos_i[:, bass.ds(b, 1), :].rearrange("p a k -> p (a k)")).then_inc(scatter_ready, 1)

            for r in range(RING):
                for_scatter(r, r)
            with dve.Fori(1, LASTB // RING, 1) as i:
                for r in range(RING):
                    gate(dve, scattered[r], i * 32)
                    for_scatter(RING * i + r, r)
            dve.wait_ge(scattered[0], 32 * (LASTB // RING))
            for_scatter(LASTB, 0)

            tiles, ends, shift = ering[:, 2, :], ering[:, 3, :], ering[:, 4, :]
            then(v.tensor_scalar(ering_i[:, 1, :], count, float(P - 1), None, ALU.add))
            then(v.tensor_scalar(ering_i[:, 2, :], ering_i[:, 1, :], 7, None, ALU.logical_shift_right))
            then(v.tensor_copy(tiles, ering_i[:, 2, :]))
            then(v.tensor_copy(ends, tiles))
            for e in range(1, NE):
                then(v.tensor_tensor(ends[:, e:e + 1], ends[:, e - 1:e], tiles[:, e:e + 1], ALU.add))
            tile_no, expert, rel, flag, taken = (sched[:, q, :] for q in range(5))
            then(v.tensor_scalar(taken[:, 0:1], ends[0:1, NE - 1:NE], -1.0, None, ALU.add))
            then(v.tensor_scalar(tile_no, iota[0:1, 0:NT], taken[:, 0:1], None, ALU.min))
            v.tensor_copy(rel, tile_no)
            then(v.memset(expert, 0.0))
            for e in range(NE - 1):
                v.tensor_scalar(flag, tile_no, ends[0:1, e:e + 1], None, ALU.is_ge)
                then(v.tensor_scalar(taken, tile_no, ends[0:1, e:e + 1], tiles[0:1, e:e + 1], ALU.is_ge, ALU.mult))
                v.tensor_tensor(expert, expert, flag, ALU.add)
                then(v.tensor_tensor(rel, rel, taken, ALU.subtract))
            v.tensor_copy(sched_i[:, 0, :], expert)
            then(v.tensor_scalar(rel, rel, float(P), None, ALU.mult))
            then(v.scalar_tensor_tensor(flag, expert, float(REGION), rel, ALU.mult, ALU.add))
            v.tensor_copy(sched_i[:, 1, :], flag).then_inc(sched_ready, 1)
            then(v.tensor_tensor(shift, ends, tiles, ALU.subtract))
            then(v.scalar_tensor_tensor(shift, shift, float(P), first_row, ALU.mult, ALU.subtract))
            for k in range(2):
                then(v.tensor_tensor(prob, mask[k][:], by_expert(shift), ALU.mult))
                then(v.tensor_reduce(red[:], prob, AX, ALU.add))
                then(v.tensor_tensor(pos[:, :, k], pos[:, :, k], red[:], ALU.add))
            then(v.tensor_copy(pos_i[:], pos[:]))

            def product(n):
                gate(dve, hidden_made, n + 1)
                gate(dve, silu_made, n + 1)
                gate(dve, h_turned, n + 1)
                v.tensor_tensor(h.rearrange("p (c n) -> p c n", c=2), s1.rearrange("p (c n) -> p c n", c=2),
                                ps[:, 2:4, 0:HH], ALU.mult).then_inc(h_ready, 1)

            def h_out(n):
                gate(dve, h_turned, n + 2)
                gate(dve, y_made, n + 1)
                v.tensor_copy(hT[0:HC].rearrange("p (a c) n -> p a (c n)", a=2), ps[0:HC, 4:6, 0:3 * P]).then_inc(hT_ready, 1)

            def y_out(r, i, n):
                gate(dve, y_made, n + 2)
                gate(dve, yb_written[r], i * 16 + 16 * NE // 2)
                v.tensor_copy(yb[:, r], ps[:, 6, 0:D]).then_inc(y_ready, 1)

            product(0)
            product(1)
            h_out(0)
            with dve.Fori(0, NT // 2 - 1, 1) as i:
                for r in range(2):
                    product(2 * i + (r + 2))
                    h_out(2 * i + (r + 1))
                    y_out(r, i, 2 * i + r)
            h_out(NT - 1)
            for n in (NT - 2, NT - 1):
                y_out(n % 2, NT // 2 - 1, n)

            def ask(b, r):
                v.tensor_copy(ring_i[:, r, :], pos_i[:, bass.ds(b, 1), :].rearrange("p a k -> p (a k)")).then_inc(comb_ready, 1)

            def combine(b, r, i):
                gate(dve, y_back[r], i * 32 + 32)
                v.scalar_tensor_tensor(acc_block(b), both[:, r, 0], gate_p[0][:, bass.ds(b, 1)], acc_block(b), ALU.mult, ALU.add).then_inc(first_gated, 1)
                gate(dve, first_gated, b + 1)
                v.scalar_tensor_tensor(acc_block(b), both[:, r, 1], gate_p[1][:, bass.ds(b, 1)], acc_block(b), ALU.mult, ALU.add).then_inc(out_ready, 1)

            for r in range(RING):
                ask(r, r)
            with dve.Fori(0, LASTB // RING - 1, 1) as i:
                for r in range(RING):
                    combine(RING * i + r, r, i)
                    gate(dve, out_ready, RING * i + (r + 1))
                    ask(RING * i + (r + RING), r)
            for r in range(RING):
                combine(LASTB - RING + r, r, LASTB // RING - 1)
                if r == 0:
                    dve.wait_ge(out_ready, LASTB - RING + 1)
                    ask(LASTB, 0)
            combine(LASTB, 0, LASTB // RING)


_OUT = ((N, D), "float32")


def kernel(x, src, dst, L0_gnn_W1, L0_gnn_b1, L0_gnn_W2, L0_gnn_b2, L0_ffn_router_w, L0_ffn_w1, L0_ffn_w2, L0_ffn_w3):
    import concourse.bacc as _bacc
    from concourse.bass_utils import run_bass_kernel_spmd as _run

    def edges(a, fill):
        flat = np.full((E_PAD,), fill, np.int32)
        flat[:E_IN] = np.asarray(a)
        return flat

    def hidden_weights(w):
        w = np.asarray(w)
        padded = np.zeros((NE, HP, D), w.dtype)
        padded[:, :HID] = w
        return np.ascontiguousarray(padded.transpose(2, 0, 1).reshape(D, NE * HP))

    def output_weights(w):
        w = np.asarray(w)
        padded = np.zeros((NE, D, HP), w.dtype)
        padded[:, :, :HID] = w
        return np.ascontiguousarray(padded.transpose(2, 0, 1).reshape(HP, NE * D))

    src_flat, dst_flat = edges(src, N), edges(dst, N)
    arrays = {
        "x": np.ascontiguousarray(x),
        "src": np.ascontiguousarray(src_flat.reshape(TILES, P).T),
        "dst": np.ascontiguousarray(dst_flat.reshape(TILES, P).T),
        "dst_spans": dst_flat.reshape(GP, GQ * GT * P),
        "W1": np.ascontiguousarray(L0_gnn_W1),
        "b1": np.ascontiguousarray(np.asarray(L0_gnn_b1).reshape(KC, P).T),
        "W2": np.ascontiguousarray(L0_gnn_W2),
        "b2": np.ascontiguousarray(L0_gnn_b2).reshape(1, D),
        "router": np.ascontiguousarray(np.asarray(L0_ffn_router_w).T),
        "w1": hidden_weights(L0_ffn_w1),
        "w3": hidden_weights(L0_ffn_w3),
        "w2": output_weights(L0_ffn_w2),
    }
    nc = _bacc.Bacc("TRN2", target_bir_lowering=False, num_devices=1, dynamic_dma_scratch_size=8192)
    args, ins = {}, {}
    for name, a in arrays.items():
        t = nc.dram_tensor(f"in_{name}", a.shape, mybir.dt.from_np(a.dtype), kind="ExternalInput")
        args[name], ins[f"in_{name}"] = t.ap(), a
    args["out"] = nc.dram_tensor("out_rows", _OUT[0], F32, kind="ExternalOutput").ap()
    build(nc, **args)
    r = _run(nc, [ins], core_ids=[0])
    return r.results[0]["out_rows"]
```
